# Optimizing a Trainium2 kernel written in Bass

```python
import numpy as np
import jax
import jax.numpy as jnp

def _softmax(x, axis=-1):
    return jax.nn.softmax(x, axis=axis)

def _gelu(x):
    return jax.nn.gelu(x, approximate=True)

def _silu(x):
    return jax.nn.silu(x)

def _sigmoid(x):
    return jax.nn.sigmoid(x)

def _layernorm(x, axis=-1, eps=1e-05):
    m = jnp.mean(x, axis=axis, keepdims=True)
    v = jnp.var(x, axis=axis, keepdims=True)
    return (x - m) / jnp.sqrt(v + eps)

def _scatter_add(tgt, idx, src, axis=0):
    return tgt.at[idx].add(src)

def _segment_sum(src, seg, n):
    return jax.ops.segment_sum(src, seg, n)
kernel_name = 'mk_pixart_seq_d4_seqx_r8_60219a'

def setup_inputs(seed: int=0):
    np.random.seed(seed)
    _w = jnp.asarray

    def _rec_inputs():
        import jax
        import jax.numpy as jnp
        _rk = jax.random.key(seed)
        x = -0.0003929 + 0.9999 * jax.random.normal(jax.random.fold_in(_rk, 1), (8, 128, 128), jnp.float32)
        _lenS = 128 - jax.random.randint(jax.random.fold_in(_rk, 7), (8,), 0, max(1, 128 // 4) + 1, jnp.int32)
        _lenS2 = 77 - jax.random.randint(jax.random.fold_in(_rk, 8), (8,), 0, max(1, 77 // 4) + 1, jnp.int32)
        _ctx_1024P = jax.random.normal(jax.random.fold_in(_rk, 11), (8, 16, 128), jnp.float32)
        _ctx_1024c = jax.random.dirichlet(jax.random.fold_in(_rk, 511), 0.3 * jnp.ones((16,), jnp.float32), (8, 77))
        _ctx_1024t = jnp.einsum('bsk,bkd->bsd', _ctx_1024c, _ctx_1024P)
        _ctx_1024t = _ctx_1024t * jax.lax.rsqrt(jnp.mean(jnp.square(_ctx_1024t)) + 1e-12) * 0.953939
        ctx_1024 = -1.39393e-06 + 0.999914 * (_ctx_1024t + 0.3 * jax.random.normal(jax.random.fold_in(_rk, 611), (8, 77, 128), jnp.float32))
        cond_1024 = -0.00920427 + 1.00102 * jax.random.normal(jax.random.fold_in(_rk, 12), (8, 128), jnp.float32)
        _validS = jnp.arange(128)[None, :] < _lenS[:, None]
        _validS2 = jnp.arange(77)[None, :] < _lenS2[:, None]
        _causal = jnp.tril(jnp.ones((128, 128), dtype=bool))
        mask_BxS2_bf1 = jnp.ones((8, 77), dtype=bool)
        mask_SxS_bk0 = jnp.logical_not(jnp.broadcast_to(_validS[0:1, :], (128, 128)))
        return (x, ctx_1024, cond_1024, mask_BxS2_bf1, mask_SxS_bk0)
    x, ctx_1024, cond_1024, mask_BxS2_bf1, mask_SxS_bk0 = _rec_inputs()

    def _L0_xcond_setup():
        import jax, jax.numpy as jnp
        import numpy as np
        EPS = 1e-05

        def _ada_ln(x, c, W_ss, b_ss):
            mu = jnp.mean(x, axis=-1, keepdims=True)
            var = jnp.mean((x - mu) ** 2, axis=-1, keepdims=True)
            h = (x - mu) / jnp.sqrt(var + EPS)
            ss = jax.nn.silu(c) @ W_ss + b_ss
            scale, bias = jnp.split(ss, 2, axis=-1)
            return (1.0 + scale)[:, None, :] * h + bias[:, None, :]
        key = jax.random.key(seed)
        ks = jax.random.split(key, 12)
        B, Lq, Lkv, H = (8, 256, 64, 128)
        s = 0.02
        return {'x_q': jax.random.normal(ks[0], (B, Lq, H), jnp.float32), 'x_kv': jax.random.normal(ks[1], (B, Lkv, H), jnp.float32), 't_vec': jax.random.normal(ks[2], (B, H), jnp.float32), 'Wq': jax.random.normal(ks[3], (H, H), jnp.float32) * s, 'bq': jnp.zeros((H,), jnp.float32), 'Wkv': jax.random.normal(ks[4], (H, 2 * H), jnp.float32) * s, 'bkv': jnp.zeros((2 * H,), jnp.float32), 'Wp': jax.random.normal(ks[5], (H, H), jnp.float32) * s, 'bp': jnp.zeros((H,), jnp.float32), 'Wss_q': jax.random.normal(ks[6], (H, 2 * H), jnp.float32) * s, 'bss_q': jnp.zeros((2 * H,), jnp.float32), 'Wss_kv': jax.random.normal(ks[7], (H, 2 * H), jnp.float32) * s, 'bss_kv': jnp.zeros((2 * H,), jnp.float32)}
    _L0_xcond_all = _L0_xcond_setup()
    _L0_xcond_in = {k: v for k, v in _L0_xcond_all.items() if k in ('Wq', 'bq', 'Wkv', 'bkv', 'Wp', 'bp', 'Wss_q', 'bss_q', 'Wss_kv', 'bss_kv')}
    del _L0_xcond_all

    def _L1_xcond_setup():
        import jax, jax.numpy as jnp
        import numpy as np
        B, N, D, H, LC = (2, 128, 128, 16, 77)
        HD = D // H
        BLOCK = 16
        ROPE_BASE = 10000.0
        EPS = 1e-05

        def _block_diff_mask(n, block_size):
            idx = np.arange(2 * n)
            q = idx[:, None]
            kv = idx[None, :]
            fq = q >= n
            fkv = kv >= n
            bq = np.where(fq, (q - n) // block_size, q // block_size)
            bkv = np.where(fkv, (kv - n) // block_size, kv // block_size)
            block_diagonal = (bq == bkv) & (fq == fkv)
            offset_block_causal = (bq > bkv) & fkv & ~fq
            block_causal = (bq >= bkv) & fq & fkv
            return jnp.asarray(block_diagonal | offset_block_causal | block_causal)

        def _rope_tables(n):
            inv_freq = 1.0 / ROPE_BASE ** (np.arange(0, HD, 2, dtype=np.float32) / HD)
            freqs = np.outer(np.arange(n, dtype=np.float32), inv_freq)
            emb = np.concatenate([freqs, freqs], axis=-1)
            cos = jnp.asarray(np.cos(emb), jnp.float32)[None, :, None, :]
            sin = jnp.asarray(np.sin(emb), jnp.float32)[None, :, None, :]
            return (cos, sin)

        def _ln(x, w):
            xf = x.astype(jnp.float32)
            mu = jnp.mean(xf, axis=-1, keepdims=True)
            var = jnp.mean(jnp.square(xf - mu), axis=-1, keepdims=True)
            y = (xf - mu) * jax.lax.rsqrt(var + EPS)
            return y * w[None, None, :]

        def _apply_rope(t, cos, sin):
            t1, t2 = jnp.split(t, 2, axis=-1)
            rot = jnp.concatenate([-t2, t1], axis=-1)
            return t * cos + rot * sin

        def _attn(q, k, v, mask):
            scale = 1.0 / np.sqrt(HD)
            s = jnp.einsum('bqhd,bkhd->bhqk', q, k) * scale
            s = jnp.where(mask, s, jnp.finfo(s.dtype).min)
            a = jax.nn.softmax(s, axis=-1)
            return jnp.einsum('bhqk,bkhd->bqhd', a, v)
        key = jax.random.key(seed)
        ks = jax.random.split(key, 16)
        w = lambda k, shp: jax.random.normal(k, shp, jnp.float32) * 0.02
        inp = {'x': jax.random.normal(ks[0], (B, 2 * N, D), jnp.float32), 'cond_global': jax.random.normal(ks[1], (B, D), jnp.float32), 'cond_tokens': jax.random.normal(ks[2], (B, LC, D), jnp.float32), 'adaLN_W': w(ks[3], (D, 9 * D)), 'adaLN_b': w(ks[4], (9 * D,)), 'norm1_w': jnp.ones((D,), jnp.float32), 'qkv_W': w(ks[5], (D, 3 * D)), 'attn_out_W': w(ks[6], (D, D)), 'normc_w': jnp.ones((D,), jnp.float32), 'cq_W': w(ks[7], (D, D)), 'ck_W': w(ks[8], (D, D)), 'cv_W': w(ks[9], (D, D)), 'co_W': w(ks[10], (D, D)), 'norm2_w': jnp.ones((D,), jnp.float32), 'mlp_W1': w(ks[11], (D, 4 * D)), 'mlp_b1': w(ks[12], (4 * D,)), 'mlp_W2': w(ks[13], (4 * D, D)), 'mlp_b2': w(ks[14], (D,)), 'cond_kv_mask': jnp.ones((B, LC), bool), 'attn_mask': _block_diff_mask(N, BLOCK)}
        return inp
    _L1_xcond_all = _L1_xcond_setup()
    _L1_xcond_in = {k: v for k, v in _L1_xcond_all.items() if k in ('adaLN_W', 'adaLN_b', 'norm1_w', 'qkv_W', 'attn_out_W', 'normc_w', 'cq_W', 'ck_W', 'cv_W', 'co_W', 'norm2_w', 'mlp_W1', 'mlp_b1', 'mlp_W2', 'mlp_b2')}
    del _L1_xcond_all

    def _L2_xcond_setup():
        import jax, jax.numpy as jnp
        import numpy as np
        LN_EPS = 1e-06

        def _ln(x):
            mu = jnp.mean(x, axis=-1, keepdims=True)
            var = jnp.var(x, axis=-1, keepdims=True)
            return (x - mu) * jax.lax.rsqrt(var + LN_EPS)
        key = jax.random.key(seed)
        H, NH = (128, 16)
        B, N, S = (4, 128, 77)
        MLP = int(H * 4.0)
        ks = jax.random.split(key, 20)
        s = 1.0 / np.sqrt(H)
        return {'x': jax.random.normal(ks[0], (B, N, H), jnp.float32), 'c': jax.random.normal(ks[1], (B, H), jnp.float32), 'context': jax.random.normal(ks[2], (B, S, H), jnp.float32), 'W_mod': jax.random.normal(ks[3], (H, 6 * H), jnp.float32) * s, 'b_mod': jnp.zeros((6 * H,), jnp.float32), 'W_qkv': jax.random.normal(ks[4], (H, 3 * H), jnp.float32) * s, 'b_qkv': jnp.zeros((3 * H,), jnp.float32), 'W_proj': jax.random.normal(ks[5], (H, H), jnp.float32) * s, 'b_proj': jnp.zeros((H,), jnp.float32), 'W_qc': jax.random.normal(ks[6], (H, H), jnp.float32) * s, 'b_qc': jnp.zeros((H,), jnp.float32), 'W_kvc': jax.random.normal(ks[7], (H, 2 * H), jnp.float32) * s, 'b_kvc': jnp.zeros((2 * H,), jnp.float32), 'W_cproj': jax.random.normal(ks[8], (H, H), jnp.float32) * s, 'b_cproj': jnp.zeros((H,), jnp.float32), 'W_mlp1': jax.random.normal(ks[9], (H, MLP), jnp.float32) * s, 'b_mlp1': jnp.zeros((MLP,), jnp.float32), 'W_mlp2': jax.random.normal(ks[10], (MLP, H), jnp.float32) * (1.0 / np.sqrt(MLP)), 'b_mlp2': jnp.zeros((H,), jnp.float32)}
    _L2_xcond_all = _L2_xcond_setup()
    _L2_xcond_in = {k: v for k, v in _L2_xcond_all.items() if k in ('W_mod', 'b_mod', 'W_qkv', 'b_qkv', 'W_proj', 'b_proj', 'W_qc', 'b_qc', 'W_kvc', 'b_kvc', 'W_cproj', 'b_cproj', 'W_mlp1', 'b_mlp1', 'W_mlp2', 'b_mlp2')}
    del _L2_xcond_all

    def _L3_xcond_setup():
        import jax, jax.numpy as jnp
        import numpy as np
        import math
        D_MODEL = 128
        N_HEADS = 16
        HEAD_DIM = D_MODEL // N_HEADS
        D_FF = 512
        EPS = 1e-05
        ROPE_BASE = 10000.0

        def _rope(t):
            L, Dh = (t.shape[1], t.shape[-1])
            half = Dh // 2
            inv_freq = 1.0 / ROPE_BASE ** (jnp.arange(half, dtype=t.dtype) / half)
            ang = jnp.arange(L, dtype=t.dtype)[:, None] * inv_freq[None, :]
            cos = jnp.cos(ang)[None, :, None, :]
            sin = jnp.sin(ang)[None, :, None, :]
            t1, t2 = (t[..., :half], t[..., half:])
            return jnp.concatenate([t1 * cos - t2 * sin, t2 * cos + t1 * sin], axis=-1)

        def _adaln(x, emb, w, b):
            e = emb[:, 0, :]
            gb = e @ w.T + b
            gamma, beta = jnp.split(gb, 2, axis=-1)
            mu = x.mean(-1, keepdims=True)
            var = x.var(-1, keepdims=True)
            xn = (x - mu) * jax.lax.rsqrt(var + EPS)
            return xn * (1.0 + gamma[:, None, :]) + beta[:, None, :]

        def _attn(q, k, v):
            scale = 1.0 / math.sqrt(HEAD_DIM)
            scores = jnp.einsum('bqhd,bkhd->bhqk', q, k) * scale
            w = jax.nn.softmax(scores, axis=-1)
            out = jnp.einsum('bhqk,bkhd->bqhd', w, v)
            B, Lq = (out.shape[0], out.shape[1])
            return out.reshape(B, Lq, D_MODEL)
        key = jax.random.key(seed)
        ks = jax.random.split(key, 24)
        s = 0.02
        inp = {'x': jax.random.normal(ks[0], (2, 256, D_MODEL), jnp.float32), 'noise_emb': jax.random.normal(ks[1], (2, 1, D_MODEL), jnp.float32), 'context': jax.random.normal(ks[2], (2, 128, D_MODEL), jnp.float32), 'ln1_w': jax.random.normal(ks[3], (2 * D_MODEL, D_MODEL), jnp.float32) * s, 'ln1_b': jax.random.normal(ks[4], (2 * D_MODEL,), jnp.float32) * s, 'ln2_w': jax.random.normal(ks[5], (2 * D_MODEL, D_MODEL), jnp.float32) * s, 'ln2_b': jax.random.normal(ks[6], (2 * D_MODEL,), jnp.float32) * s, 'ln3_w': jax.random.normal(ks[7], (2 * D_MODEL, D_MODEL), jnp.float32) * s, 'ln3_b': jax.random.normal(ks[8], (2 * D_MODEL,), jnp.float32) * s, 'qkv_w': jax.random.normal(ks[9], (3 * D_MODEL, D_MODEL), jnp.float32) * s, 'sa_out_w': jax.random.normal(ks[10], (D_MODEL, D_MODEL), jnp.float32) * s, 'q_w': jax.random.normal(ks[11], (D_MODEL, D_MODEL), jnp.float32) * s, 'k_w': jax.random.normal(ks[12], (D_MODEL, D_MODEL), jnp.float32) * s, 'v_w': jax.random.normal(ks[13], (D_MODEL, D_MODEL), jnp.float32) * s, 'ca_out_w': jax.random.normal(ks[14], (D_MODEL, D_MODEL), jnp.float32) * s, 'ffn_w1': jax.random.normal(ks[15], (D_FF, D_MODEL), jnp.float32) * s, 'ffn_b1': jax.random.normal(ks[16], (D_FF,), jnp.float32) * s, 'ffn_w2': jax.random.normal(ks[17], (D_MODEL, D_FF), jnp.float32) * s, 'ffn_b2': jax.random.normal(ks[18], (D_MODEL,), jnp.float32) * s}
        return inp
    _L3_xcond_all = _L3_xcond_setup()
    _L3_xcond_in = {k: v for k, v in _L3_xcond_all.items() if k in ('ln1_w', 'ln1_b', 'ln2_w', 'ln2_b', 'ln3_w', 'ln3_b', 'qkv_w', 'sa_out_w', 'q_w', 'k_w', 'v_w', 'ca_out_w', 'ffn_w1', 'ffn_b1', 'ffn_w2', 'ffn_b2')}
    del _L3_xcond_all
    return {'x': x, 'ctx_1024': ctx_1024, 'cond_1024': cond_1024, 'mask_BxS2_bf1': mask_BxS2_bf1, 'mask_SxS_bk0': mask_SxS_bk0, 'L0_xcond_Wq': _L0_xcond_in['Wq'], 'L0_xcond_bq': _L0_xcond_in['bq'], 'L0_xcond_Wkv': _L0_xcond_in['Wkv'], 'L0_xcond_bkv': _L0_xcond_in['bkv'], 'L0_xcond_Wp': _L0_xcond_in['Wp'], 'L0_xcond_bp': _L0_xcond_in['bp'], 'L0_xcond_Wss_q': _L0_xcond_in['Wss_q'], 'L0_xcond_bss_q': _L0_xcond_in['bss_q'], 'L0_xcond_Wss_kv': _L0_xcond_in['Wss_kv'], 'L0_xcond_bss_kv': _L0_xcond_in['bss_kv'], 'L1_xcond_adaLN_W': _L1_xcond_in['adaLN_W'], 'L1_xcond_adaLN_b': _L1_xcond_in['adaLN_b'], 'L1_xcond_norm1_w': _L1_xcond_in['norm1_w'], 'L1_xcond_qkv_W': _L1_xcond_in['qkv_W'], 'L1_xcond_attn_out_W': _L1_xcond_in['attn_out_W'], 'L1_xcond_normc_w': _L1_xcond_in['normc_w'], 'L1_xcond_cq_W': _L1_xcond_in['cq_W'], 'L1_xcond_ck_W': _L1_xcond_in['ck_W'], 'L1_xcond_cv_W': _L1_xcond_in['cv_W'], 'L1_xcond_co_W': _L1_xcond_in['co_W'], 'L1_xcond_norm2_w': _L1_xcond_in['norm2_w'], 'L1_xcond_mlp_W1': _L1_xcond_in['mlp_W1'], 'L1_xcond_mlp_b1': _L1_xcond_in['mlp_b1'], 'L1_xcond_mlp_W2': _L1_xcond_in['mlp_W2'], 'L1_xcond_mlp_b2': _L1_xcond_in['mlp_b2'], 'L2_xcond_W_mod': _L2_xcond_in['W_mod'], 'L2_xcond_b_mod': _L2_xcond_in['b_mod'], 'L2_xcond_W_qkv': _L2_xcond_in['W_qkv'], 'L2_xcond_b_qkv': _L2_xcond_in['b_qkv'], 'L2_xcond_W_proj': _L2_xcond_in['W_proj'], 'L2_xcond_b_proj': _L2_xcond_in['b_proj'], 'L2_xcond_W_qc': _L2_xcond_in['W_qc'], 'L2_xcond_b_qc': _L2_xcond_in['b_qc'], 'L2_xcond_W_kvc': _L2_xcond_in['W_kvc'], 'L2_xcond_b_kvc': _L2_xcond_in['b_kvc'], 'L2_xcond_W_cproj': _L2_xcond_in['W_cproj'], 'L2_xcond_b_cproj': _L2_xcond_in['b_cproj'], 'L2_xcond_W_mlp1': _L2_xcond_in['W_mlp1'], 'L2_xcond_b_mlp1': _L2_xcond_in['b_mlp1'], 'L2_xcond_W_mlp2': _L2_xcond_in['W_mlp2'], 'L2_xcond_b_mlp2': _L2_xcond_in['b_mlp2'], 'L3_xcond_ln1_w': _L3_xcond_in['ln1_w'], 'L3_xcond_ln1_b': _L3_xcond_in['ln1_b'], 'L3_xcond_ln2_w': _L3_xcond_in['ln2_w'], 'L3_xcond_ln2_b': _L3_xcond_in['ln2_b'], 'L3_xcond_ln3_w': _L3_xcond_in['ln3_w'], 'L3_xcond_ln3_b': _L3_xcond_in['ln3_b'], 'L3_xcond_qkv_w': _L3_xcond_in['qkv_w'], 'L3_xcond_sa_out_w': _L3_xcond_in['sa_out_w'], 'L3_xcond_q_w': _L3_xcond_in['q_w'], 'L3_xcond_k_w': _L3_xcond_in['k_w'], 'L3_xcond_v_w': _L3_xcond_in['v_w'], 'L3_xcond_ca_out_w': _L3_xcond_in['ca_out_w'], 'L3_xcond_ffn_w1': _L3_xcond_in['ffn_w1'], 'L3_xcond_ffn_b1': _L3_xcond_in['ffn_b1'], 'L3_xcond_ffn_w2': _L3_xcond_in['ffn_w2'], 'L3_xcond_ffn_b2': _L3_xcond_in['ffn_b2']}

def reference(x, ctx_1024, cond_1024, mask_BxS2_bf1, mask_SxS_bk0, L0_xcond_Wq, L0_xcond_bq, L0_xcond_Wkv, L0_xcond_bkv, L0_xcond_Wp, L0_xcond_bp, L0_xcond_Wss_q, L0_xcond_bss_q, L0_xcond_Wss_kv, L0_xcond_bss_kv, L1_xcond_adaLN_W, L1_xcond_adaLN_b, L1_xcond_norm1_w, L1_xcond_qkv_W, L1_xcond_attn_out_W, L1_xcond_normc_w, L1_xcond_cq_W, L1_xcond_ck_W, L1_xcond_cv_W, L1_xcond_co_W, L1_xcond_norm2_w, L1_xcond_mlp_W1, L1_xcond_mlp_b1, L1_xcond_mlp_W2, L1_xcond_mlp_b2, L2_xcond_W_mod, L2_xcond_b_mod, L2_xcond_W_qkv, L2_xcond_b_qkv, L2_xcond_W_proj, L2_xcond_b_proj, L2_xcond_W_qc, L2_xcond_b_qc, L2_xcond_W_kvc, L2_xcond_b_kvc, L2_xcond_W_cproj, L2_xcond_b_cproj, L2_xcond_W_mlp1, L2_xcond_b_mlp1, L2_xcond_W_mlp2, L2_xcond_b_mlp2, L3_xcond_ln1_w, L3_xcond_ln1_b, L3_xcond_ln2_w, L3_xcond_ln2_b, L3_xcond_ln3_w, L3_xcond_ln3_b, L3_xcond_qkv_w, L3_xcond_sa_out_w, L3_xcond_q_w, L3_xcond_k_w, L3_xcond_v_w, L3_xcond_ca_out_w, L3_xcond_ffn_w1, L3_xcond_ffn_b1, L3_xcond_ffn_w2, L3_xcond_ffn_b2):
    import jax
    import jax.numpy as jnp

    def _L0_xcond_ref(x_q, x_kv, t_vec, Wq, bq, Wkv, bkv, Wp, bp, Wss_q, bss_q, Wss_kv, bss_kv):
        import jax, jax.numpy as jnp
        import numpy as np
        EPS = 1e-05

        def _ada_ln(x, c, W_ss, b_ss):
            mu = jnp.mean(x, axis=-1, keepdims=True)
            var = jnp.mean((x - mu) ** 2, axis=-1, keepdims=True)
            h = (x - mu) / jnp.sqrt(var + EPS)
            ss = jax.nn.silu(c) @ W_ss + b_ss
            scale, bias = jnp.split(ss, 2, axis=-1)
            return (1.0 + scale)[:, None, :] * h + bias[:, None, :]
        B, Lq, H = x_q.shape
        Lkv = x_kv.shape[1]
        nh = 16
        dh = H // nh
        xq = _ada_ln(x_q, t_vec, Wss_q, bss_q)
        xkv = _ada_ln(x_kv, t_vec, Wss_kv, bss_kv)
        q = (xq @ Wq + bq).reshape(B, Lq, nh, dh)
        kv = (xkv @ Wkv + bkv).reshape(B, Lkv, 2, nh, dh)
        k = kv[:, :, 0]
        v = kv[:, :, 1]
        scores = jnp.einsum('bqhd,bkhd->bhqk', q, k) / jnp.sqrt(jnp.float32(dh))
        attn = jax.nn.softmax(scores, axis=-1)
        out = jnp.einsum('bhqk,bkhd->bqhd', attn, v).reshape(B, Lq, H)
        return x_q + (out @ Wp + bp)

    def _L1_xcond_ref(x, cond_global, cond_tokens, adaLN_W, adaLN_b, norm1_w, qkv_W, attn_out_W, normc_w, cq_W, ck_W, cv_W, co_W, norm2_w, mlp_W1, mlp_b1, mlp_W2, mlp_b2, cond_kv_mask, attn_mask):
        import jax, jax.numpy as jnp
        import numpy as np
        B, N, D, H, LC = (2, 128, 128, 16, 77)
        HD = D // H
        BLOCK = 16
        ROPE_BASE = 10000.0
        EPS = 1e-05

        def _block_diff_mask(n, block_size):
            idx = np.arange(2 * n)
            q = idx[:, None]
            kv = idx[None, :]
            fq = q >= n
            fkv = kv >= n
            bq = np.where(fq, (q - n) // block_size, q // block_size)
            bkv = np.where(fkv, (kv - n) // block_size, kv // block_size)
            block_diagonal = (bq == bkv) & (fq == fkv)
            offset_block_causal = (bq > bkv) & fkv & ~fq
            block_causal = (bq >= bkv) & fq & fkv
            return jnp.asarray(block_diagonal | offset_block_causal | block_causal)

        def _rope_tables(n):
            inv_freq = 1.0 / ROPE_BASE ** (np.arange(0, HD, 2, dtype=np.float32) / HD)
            freqs = np.outer(np.arange(n, dtype=np.float32), inv_freq)
            emb = np.concatenate([freqs, freqs], axis=-1)
            cos = jnp.asarray(np.cos(emb), jnp.float32)[None, :, None, :]
            sin = jnp.asarray(np.sin(emb), jnp.float32)[None, :, None, :]
            return (cos, sin)

        def _ln(x, w):
            xf = x.astype(jnp.float32)
            mu = jnp.mean(xf, axis=-1, keepdims=True)
            var = jnp.mean(jnp.square(xf - mu), axis=-1, keepdims=True)
            y = (xf - mu) * jax.lax.rsqrt(var + EPS)
            return y * w[None, None, :]

        def _apply_rope(t, cos, sin):
            t1, t2 = jnp.split(t, 2, axis=-1)
            rot = jnp.concatenate([-t2, t1], axis=-1)
            return t * cos + rot * sin

        def _attn(q, k, v, mask):
            scale = 1.0 / np.sqrt(HD)
            s = jnp.einsum('bqhd,bkhd->bhqk', q, k) * scale
            s = jnp.where(mask, s, jnp.finfo(s.dtype).min)
            a = jax.nn.softmax(s, axis=-1)
            return jnp.einsum('bhqk,bkhd->bqhd', a, v)
        b, s, d = x.shape
        n = s // 2
        mod = (cond_global @ adaLN_W + adaLN_b)[:, None, :]
        sh_msa, sc_msa, g_msa, sh_x, sc_x, g_x, sh_mlp, sc_mlp, g_mlp = jnp.split(mod, 9, axis=-1)
        x_norm = _ln(x, norm1_w) * (1 + sc_msa) + sh_msa
        cos, sin = _rope_tables(n)

        def qkv(h):
            t = (h @ qkv_W).reshape(b, n, 3, H, HD)
            q, k, v = (t[:, :, 0], t[:, :, 1], t[:, :, 2])
            return (_apply_rope(q, cos, sin), _apply_rope(k, cos, sin), v)
        q1, k1, v1 = qkv(x_norm[:, :n])
        q2, k2, v2 = qkv(x_norm[:, n:])
        q = jnp.concatenate([q1, q2], axis=1)
        k = jnp.concatenate([k1, k2], axis=1)
        v = jnp.concatenate([v1, v2], axis=1)
        self_out = _attn(q, k, v, attn_mask[None, None]).reshape(b, s, d) @ attn_out_W
        x = x + g_msa * self_out
        xc = _ln(x, normc_w) * (1 + sc_x) + sh_x
        qc = (xc @ cq_W).reshape(b, s, H, HD)
        kc = (cond_tokens @ ck_W).reshape(b, LC, H, HD)
        vc = (cond_tokens @ cv_W).reshape(b, LC, H, HD)
        cross = _attn(qc, kc, vc, cond_kv_mask[:, None, None, :]).reshape(b, s, d) @ co_W
        x = x + g_x * cross
        xm = _ln(x, norm2_w) * (1 + sc_mlp) + sh_mlp
        h = jax.nn.gelu(xm @ mlp_W1 + mlp_b1, approximate=True)
        mlp_out = h @ mlp_W2 + mlp_b2
        return x + g_mlp * mlp_out

    def _L2_xcond_ref(x, c, context, W_mod, b_mod, W_qkv, b_qkv, W_proj, b_proj, W_qc, b_qc, W_kvc, b_kvc, W_cproj, b_cproj, W_mlp1, b_mlp1, W_mlp2, b_mlp2):
        import jax, jax.numpy as jnp
        import numpy as np
        LN_EPS = 1e-06

        def _ln(x):
            mu = jnp.mean(x, axis=-1, keepdims=True)
            var = jnp.var(x, axis=-1, keepdims=True)
            return (x - mu) * jax.lax.rsqrt(var + LN_EPS)
        B, N, H = x.shape
        NH = 16
        hd = H // NH
        scale = hd ** (-0.5)
        c_proj = jax.nn.silu(c) @ W_mod + b_mod
        shift_a, scale_a, gate_a, shift_m, scale_m, gate_m = jnp.split(c_proj, 6, axis=-1)

        def modulate(t, shift, sc):
            return t * (1 + sc[:, None]) + shift[:, None]
        x_norm = modulate(_ln(x), shift_a, scale_a)
        qkv = x_norm @ W_qkv + b_qkv
        q, k, v = jnp.split(qkv, 3, axis=-1)
        q = q.reshape(B, N, NH, hd).transpose(0, 2, 1, 3)
        k = k.reshape(B, N, NH, hd).transpose(0, 2, 1, 3)
        v = v.reshape(B, N, NH, hd).transpose(0, 2, 1, 3)
        attn_w = jax.nn.softmax(jnp.einsum('bhqd,bhkd->bhqk', q, k) * scale, axis=-1)
        attn_out = jnp.einsum('bhqk,bhkd->bhqd', attn_w, v)
        attn_out = attn_out.transpose(0, 2, 1, 3).reshape(B, N, H)
        attn_out = attn_out @ W_proj + b_proj
        x = x + gate_a[:, None] * attn_out
        S = context.shape[1]
        q_c = _ln(x) @ W_qc + b_qc
        kv_c = _ln(context) @ W_kvc + b_kvc
        k_c, v_c = jnp.split(kv_c, 2, axis=-1)
        q_c = q_c.reshape(B, N, NH, hd).transpose(0, 2, 1, 3)
        k_c = k_c.reshape(B, S, NH, hd).transpose(0, 2, 1, 3)
        v_c = v_c.reshape(B, S, NH, hd).transpose(0, 2, 1, 3)
        c_attn_w = jax.nn.softmax(jnp.einsum('bhqd,bhsd->bhqs', q_c, k_c) * scale, axis=-1)
        c_attn_out = jnp.einsum('bhqs,bhsd->bhqd', c_attn_w, v_c)
        c_attn_out = c_attn_out.transpose(0, 2, 1, 3).reshape(B, N, H)
        c_attn_out = c_attn_out @ W_cproj + b_cproj
        x = x + c_attn_out
        x_norm2 = modulate(_ln(x), shift_m, scale_m)
        h = jax.nn.gelu(x_norm2 @ W_mlp1 + b_mlp1)
        h = h @ W_mlp2 + b_mlp2
        x = x + gate_m[:, None] * h
        return x

    def _L3_xcond_ref(x, noise_emb, context, ln1_w, ln1_b, ln2_w, ln2_b, ln3_w, ln3_b, qkv_w, sa_out_w, q_w, k_w, v_w, ca_out_w, ffn_w1, ffn_b1, ffn_w2, ffn_b2):
        import jax, jax.numpy as jnp
        import numpy as np
        import math
        D_MODEL = 128
        N_HEADS = 16
        HEAD_DIM = D_MODEL // N_HEADS
        D_FF = 512
        EPS = 1e-05
        ROPE_BASE = 10000.0

        def _rope(t):
            L, Dh = (t.shape[1], t.shape[-1])
            half = Dh // 2
            inv_freq = 1.0 / ROPE_BASE ** (jnp.arange(half, dtype=t.dtype) / half)
            ang = jnp.arange(L, dtype=t.dtype)[:, None] * inv_freq[None, :]
            cos = jnp.cos(ang)[None, :, None, :]
            sin = jnp.sin(ang)[None, :, None, :]
            t1, t2 = (t[..., :half], t[..., half:])
            return jnp.concatenate([t1 * cos - t2 * sin, t2 * cos + t1 * sin], axis=-1)

        def _adaln(x, emb, w, b):
            e = emb[:, 0, :]
            gb = e @ w.T + b
            gamma, beta = jnp.split(gb, 2, axis=-1)
            mu = x.mean(-1, keepdims=True)
            var = x.var(-1, keepdims=True)
            xn = (x - mu) * jax.lax.rsqrt(var + EPS)
            return xn * (1.0 + gamma[:, None, :]) + beta[:, None, :]

        def _attn(q, k, v):
            scale = 1.0 / math.sqrt(HEAD_DIM)
            scores = jnp.einsum('bqhd,bkhd->bhqk', q, k) * scale
            w = jax.nn.softmax(scores, axis=-1)
            out = jnp.einsum('bhqk,bkhd->bqhd', w, v)
            B, Lq = (out.shape[0], out.shape[1])
            return out.reshape(B, Lq, D_MODEL)
        B, L, D = x.shape
        L_ctx = context.shape[1]
        res = x
        xn = _adaln(x, noise_emb, ln1_w, ln1_b)
        qkv = xn @ qkv_w.T
        q, k, v = jnp.split(qkv, 3, axis=-1)
        q = _rope(q.reshape(B, L, N_HEADS, HEAD_DIM))
        k = _rope(k.reshape(B, L, N_HEADS, HEAD_DIM))
        v = v.reshape(B, L, N_HEADS, HEAD_DIM)
        sa = _attn(q, k, v) @ sa_out_w.T
        x = res + sa
        res = x
        xn = _adaln(x, noise_emb, ln2_w, ln2_b)
        q = _rope((xn @ q_w.T).reshape(B, L, N_HEADS, HEAD_DIM))
        k = _rope((context @ k_w.T).reshape(B, L_ctx, N_HEADS, HEAD_DIM))
        v = (context @ v_w.T).reshape(B, L_ctx, N_HEADS, HEAD_DIM)
        ca = _attn(q, k, v) @ ca_out_w.T
        x = res + ca
        res = x
        xn = _adaln(x, noise_emb, ln3_w, ln3_b)
        h = jax.nn.gelu(xn @ ffn_w1.T + ffn_b1, approximate=False)
        x = res + (h @ ffn_w2.T + ffn_b2)
        return x
    x = _L0_xcond_ref(x, ctx_1024, cond_1024, L0_xcond_Wq, L0_xcond_bq, L0_xcond_Wkv, L0_xcond_bkv, L0_xcond_Wp, L0_xcond_bp, L0_xcond_Wss_q, L0_xcond_bss_q, L0_xcond_Wss_kv, L0_xcond_bss_kv)
    x = _L1_xcond_ref(x, cond_1024, ctx_1024, L1_xcond_adaLN_W, L1_xcond_adaLN_b, L1_xcond_norm1_w, L1_xcond_qkv_W, L1_xcond_attn_out_W, L1_xcond_normc_w, L1_xcond_cq_W, L1_xcond_ck_W, L1_xcond_cv_W, L1_xcond_co_W, L1_xcond_norm2_w, L1_xcond_mlp_W1, L1_xcond_mlp_b1, L1_xcond_mlp_W2, L1_xcond_mlp_b2, mask_BxS2_bf1, mask_SxS_bk0)
    x = _L2_xcond_ref(x, cond_1024, ctx_1024, L2_xcond_W_mod, L2_xcond_b_mod, L2_xcond_W_qkv, L2_xcond_b_qkv, L2_xcond_W_proj, L2_xcond_b_proj, L2_xcond_W_qc, L2_xcond_b_qc, L2_xcond_W_kvc, L2_xcond_b_kvc, L2_xcond_W_cproj, L2_xcond_b_cproj, L2_xcond_W_mlp1, L2_xcond_b_mlp1, L2_xcond_W_mlp2, L2_xcond_b_mlp2)
    x = _L3_xcond_ref(x, cond_1024[:, None, :], ctx_1024, L3_xcond_ln1_w, L3_xcond_ln1_b, L3_xcond_ln2_w, L3_xcond_ln2_b, L3_xcond_ln3_w, L3_xcond_ln3_b, L3_xcond_qkv_w, L3_xcond_sa_out_w, L3_xcond_q_w, L3_xcond_k_w, L3_xcond_v_w, L3_xcond_ca_out_w, L3_xcond_ffn_w1, L3_xcond_ffn_b1, L3_xcond_ffn_w2, L3_xcond_ffn_b2)
    return x

_drawn_inputs = setup_inputs


def setup_inputs(seed=0):
    import zlib

    import numpy as np

    out = dict(_drawn_inputs(seed))
    spreads = {'L0_xcond_bq': (0.0, 2.0),
     'L0_xcond_bkv': (0.0, 0.351),
     'L0_xcond_bp': (0.0, 0.1),
     'L0_xcond_bss_q': (0.0, 2.0),
     'L0_xcond_bss_kv': (0.0, 0.8),
     'L1_xcond_norm1_w': (1.0, 0.6),
     'L1_xcond_normc_w': (1.0, 0.6),
     'L1_xcond_norm2_w': (1.0, 0.6),
     'L2_xcond_b_mod': (0.0, 0.286),
     'L2_xcond_b_qkv': (0.0, 0.8),
     'L2_xcond_b_proj': (0.0, 0.8),
     'L2_xcond_b_qc': (0.0, 2.0),
     'L2_xcond_b_kvc': (0.0, 0.503),
     'L2_xcond_b_cproj': (0.0, 0.493),
     'L2_xcond_b_mlp1': (0.0, 0.8),
     'L2_xcond_b_mlp2': (0.0, 0.739)}
    factors = {'L0_xcond_Wq': 8.0,
     'L0_xcond_Wss_q': 8.0,
     'L0_xcond_Wss_kv': 6.887,
     'L1_xcond_adaLN_W': 3.818,
     'L1_xcond_adaLN_b': 8.0,
     'L1_xcond_qkv_W': 7.611,
     'L1_xcond_attn_out_W': 6.986,
     'L1_xcond_cq_W': 8.0,
     'L1_xcond_ck_W': 8.0,
     'L1_xcond_cv_W': 8.0,
     'L1_xcond_co_W': 8.0,
     'L1_xcond_mlp_W1': 5.347,
     'L1_xcond_mlp_b1': 8.0,
     'L1_xcond_mlp_W2': 5.232,
     'L1_xcond_mlp_b2': 8.0,
     'L3_xcond_ln1_w': 24.23,
     'L3_xcond_ln1_b': 64.0,
     'L3_xcond_ln2_w': 8.0,
     'L3_xcond_ln2_b': 32.556,
     'L3_xcond_ln3_w': 19.692,
     'L3_xcond_ln3_b': 64.0,
     'L3_xcond_q_w': 8.0,
     'L3_xcond_k_w': 8.0,
     'L3_xcond_v_w': 3.232,
     'L3_xcond_ca_out_w': 3.005,
     'L3_xcond_ffn_b1': 64.0,
     'L3_xcond_ffn_b2': 19.029,
     'L3_xcond_qkv_w': 3.819,
     'L3_xcond_sa_out_w': 3.763,
     'L3_xcond_ffn_w1': 3.509,
     'L3_xcond_ffn_w2': 3.239}
    for name, (base, spread) in spreads.items():
        noise = np.random.default_rng([zlib.crc32(name.encode()), seed]).standard_normal(out[name].shape)
        drawn = base * np.exp(spread * noise) if base else spread * noise
        out[name] = jnp.asarray(drawn.astype(out[name].dtype))
    for name, factor in factors.items():
        out[name] = (out[name] * factor).astype(out[name].dtype)
    return out
```

```python
from contextlib import ExitStack

import numpy as np

import concourse.bass as bass
from concourse import mybir

F32 = mybir.dt.float32
BF16 = mybir.dt.bfloat16
ALU = mybir.AluOpType
ACT = mybir.ActivationFunctionType
AX_X = mybir.AxisListType.X

P = 128
B, T, D = 8, 128, 128
TC = 77
H, HD = 16, 8
NCH = 2
CB = B // NCH
CW = CB * T
XW = CB * TC
FF = 4
SCALE = float(HD) ** -0.5
BIG = float(2.0 ** 100)
EXP_LN_SET = "natural_log_exp_and_others"

ATTN = [(0, False), (1, True), (1, False), (2, True), (2, False), (3, True), (3, False)]
NA = len(ATTN)
NE = NA * NCH
QUADS = 4
PHASE_QUADS = CB * QUADS

MODS = ["L0q", "L0kv", "L1sa", "L1x", "L1m", "L2a", "L2m", "L3n1", "L3n2", "L3n3"]
GATES = ["L1sa", "L1x", "L1m", "L2a", "L2m"]
NM, NG = len(MODS), len(GATES)
MOD_OF_SILU = ["L0q", "L0kv", "L2a", "L2m"]

BCOLS = ["zero", "L0bq", "L0bk", "L0bv", "L0bp", "L2bq", "L2bk", "L2bv", "L2bproj", "L2bqc", "L2bkc", "L2bvc", "L2bcp",
         "L1b2", "L2b2", "L3b2"] + [f"L{l}b1_{j}" for l in (1, 2, 3) for j in range(FF)]
BC = {n: i for i, n in enumerate(BCOLS)}
NBC = len(BCOLS)

WBLOCKS = {
    0: ["q", "k", "v", "o"],
    1: ["sq", "sqr", "sk", "skr", "sv", "so", "xq", "xk", "xv", "xo"] + [f"up{j}" for j in range(FF)] + [f"dn{j}" for j in range(FF)],
    2: ["sq", "sk", "sv", "so", "xq", "xk", "xv", "xo"] + [f"up{j}" for j in range(FF)] + [f"dn{j}" for j in range(FF)],
    3: ["sq", "sqr", "sk", "skr", "sv", "so", "xq", "xqr", "xk", "xkr", "xv", "xo"] + [f"up{j}" for j in range(FF)] + [f"dn{j}" for j in range(FF)],
}
WCOL = {}
for _l in WBLOCKS:
    for _n in WBLOCKS[_l]:
        WCOL[(_l, _n)] = 128 * len(WCOL)
NW = 128 * len(WCOL)
WSPAN = {l: (WCOL[(l, WBLOCKS[l][0])], WCOL[(l, WBLOCKS[l][-1])] + 128) for l in WBLOCKS}

CONSTS = {"center": 128, "mean": 128, "ident": 128, "ones": 128, "headones": 128, "headmask": 4, "groupmask": 4,
          "cos": 128, "sin": 128, "cos2": 128, "sin2": 128}
CCOL, NC = {}, 0
for _n, _w in CONSTS.items():
    CCOL[_n] = (NC, NC + _w)
    NC += _w


def dense_steps(f):
    a, c = divmod(f, NCH)
    steps = []

    def norm(src, mod, eps):
        steps.extend([dict(kind="center", src=src, c=c), dict(kind="var", src=src, mod=mod, eps=eps, c=c), None])

    def proj(dst, layer, name, mode, src="xn", width=CW, **more):
        steps.append(dict(kind="proj", dst=dst, w=(layer, name), mode=mode, src=src, width=width, c=c, **more))
        if mode == "rope":
            steps.append(dict(kind="proj", dst=dst, w=(layer, name + "r"), mode="rope2", src=src, width=width, c=c, **more))

    def post(a_done):
        layer, own = ATTN[a_done]
        gate = {(1, True): "L1sa", (1, False): "L1x", (2, True): "L2a"}.get((layer, own))
        w = (layer, "o" if layer == 0 else "so" if own else "xo")
        steps.append(dict(kind="post", w=w, gate=gate, bias=f"post{a_done}", c=c))

    def mlp(layer, mod, gate):
        norm("x", mod, 1e-6 if layer == 2 else 1e-5)
        steps.extend(dict(kind="up", layer=layer, j=j, c=c) for j in range(FF))
        steps.append(dict(kind="gelu", layer=layer, c=c))
        steps.append(dict(kind="down", layer=layer, gate=gate, bias=f"mlp{layer}", c=c))

    if a > 0:
        post(a - 1)
    if a == 3:
        mlp(1, "L1m", "L1m")
    if a == 5:
        mlp(2, "L2m", "L2m")
    if a == NA:
        mlp(3, "L3n3", None)
        return steps
    layer, own = ATTN[a]
    norm("x", {0: "L0q", 1: "L1sa", 2: "L1x", 3: "L2a", 4: None, 5: "L3n1", 6: "L3n2"}[a], 1e-6 if layer == 2 else 1e-5)
    if own:
        if layer == 2:
            proj("q", 2, "sq", "bias", bias="L2bq")
            proj("k", 2, "sk", "bias", bias="L2bk")
        else:
            tabs = ("cosq", "sinq", "cos2", "sin2") if layer == 1 else ("cos", "sin", "cos", "sin")
            proj("q", layer, "sq", "rope", tabs=tabs[0:2], period=T)
            proj("k", layer, "sk", "rope", tabs=tabs[2:4], period=T)
        steps.append(dict(kind="v", w=(layer, "sv"), src="xn", n=T, c=c))
    else:
        if layer == 0:
            proj("q", 0, "q", "bias", bias="L0bq")
            norm("ctx", "L0kv", 1e-5)
            proj("k", 0, "k", "bias", bias="L0bk", width=XW)
        elif layer == 1:
            proj("q", 1, "xq", "any")
            proj("k", 1, "xk", "bias", src="ctx", bias="zero", width=XW)
        elif layer == 2:
            proj("q", 2, "xq", "bias", bias="L2bqc")
            norm("ctx", None, 1e-6)
            proj("k", 2, "xk", "bias", bias="L2bkc", width=XW)
        else:
            proj("q", 3, "xq", "rope", tabs=("cos", "sin"), period=T)
            proj("k", 3, "xk", "rope", src="ctx", tabs=("cos", "sin"), width=XW, period=TC)
        src = "xn" if layer in (0, 2) else "ctx"
        steps.append(dict(kind="v", w=(layer, "v" if layer == 0 else "xv"), src=src, n=TC, c=c))
    return steps


FIRST_SLOT = 4


def plan():
    count = dict(use=0, norm=0, rope=0, qraw=0, kraw=0, post=0, mlp=0, up=0)
    posts = [0] * NCH
    lists = []
    xn_reader = -1
    for f in range(NE + NCH):
        steps = dense_steps(f)
        slots = [[] for _ in range(PHASE_QUADS)]
        for at, s in enumerate(steps):
            if s is None:
                continue
            slots[FIRST_SLOT + at * (PHASE_QUADS - FIRST_SLOT) // len(steps)].append(s)
            s["phase"] = f
            kind = s["kind"]
            if kind != "gelu":
                s["use"] = count["use"]
                count["use"] += 1
            s["norm"] = count["norm"] - (kind == "var")
            s["xn_reader"] = xn_reader
            if kind == "center":
                count["norm"] += 1
                s["x_posts"] = count["post"]
            if kind == "up" or s.get("src") == "xn":
                xn_reader = s["use"]
            if s.get("mode") in ("rope", "rope2"):
                s["rope"] = count["rope"]
                count["rope"] += s["mode"] == "rope2"
            if kind == "proj" and s["mode"] in ("bias", "any"):
                s["raw"] = count[s["dst"] + "raw"]
                count[s["dst"] + "raw"] += 1
            if kind in ("post", "down"):
                s["post"] = count["post"]
                count["post"] += 1
                posts[s["c"]] = count["post"]
            s["mlp"] = count["mlp"]
            count["mlp"] += kind == "down"
        lists.append(slots)
    return lists, posts


def blocks_kernel(nc, xT, ctxT, condT, wmod, bmod, nw, weights, bcols, consts, mask, maskT, cmaskT, cmask, outT):
    lists, last_posts = plan()
    with ExitStack() as stack:
        def sb(name, shape, dt=F32):
            return stack.enter_context(nc.sbuf_tensor(name, shape, dt))

        def ps(name):
            return stack.enter_context(nc.psum_tensor(name, [P, 512], F32))

        def sem(name):
            return stack.enter_context(nc.semaphore(name))

        x = sb("x", [P, B * T])
        ctx = sb("ctx", [P, B * TC])
        cond = sb("cond", [P, B])
        wm = sb("wm", [P, (2 * NM + NG) * 128])
        bm = sb("bm", [P, 2 * NM + NG])
        nwt = sb("nwt", [P, NM])
        w = sb("w", [P, NW])
        bc = sb("bc", [P, NBC])
        cst = sb("cst", [P, NC])
        m8 = sb("m8", [P, T], mybir.dt.uint8)
        mT8 = sb("mT8", [P, T], mybir.dt.uint8)
        cmT8 = sb("cmT8", [TC, B], mybir.dt.uint8)
        cm8 = sb("cm8", [P, B * TC], mybir.dt.uint8)
        silu = sb("silu", [P, B])
        mod = sb("mod", [P, 2 * NM + NG, B])
        pbias = sb("pbias", [P, NA + 3, B])
        pcol = sb("pcol", [P, 3])
        epst = sb("epst", [P, 2])
        mf = sb("mf", [P, T])
        mTf = sb("mTf", [P, T])
        cmTf = sb("cmTf", [TC, B])
        cmf = sb("cmf", [P, B, TC])
        anyq = sb("anyq", [P, T])
        cosq = sb("cosq", [P, T])
        sinq = sb("sinq", [P, T])
        anyc = sb("anyc", [P, B])
        noanyc = sb("noanyc", [P, B])
        anyr = sb("anyr", [P, 1])
        noany = sb("noany", [P, 1])
        mb = sb("mb", [P, T], BF16)
        cb = sb("cb", [P, B, TC], BF16)
        identb = sb("identb", [P, 128], BF16)
        onesb = sb("onesb", [P, 128], BF16)
        xc = sb("xc", [P, CW])
        sq = sb("sq", [P, CW])
        lnv = sb("lnv", [P, CW])
        rstd = sb("rstd", [P, CW])
        xhat = sb("xhat", [P, CW])
        xn = sb("xn", [P, CW])
        ropea = sb("ropea", [P, CW])
        ropeb = sb("ropeb", [P, CW])
        qraw = sb("qraw", [P, CW])
        kraw = sb("kraw", [P, CW])
        delta = sb("delta", [P, CW])
        hid = sb("hid", [P, FF, CW])
        qz = [sb(f"qz{c}", [P, QUADS, CW]) for c in range(NCH)]
        kbd = [sb(f"kbd{c}", [P, 4, CW]) for c in range(NCH)]
        vpad = [sb(f"vpad{c}", [P, CB, 4, 4, 32]) for c in range(NCH)]
        oT = [sb(f"oT{c}", [P, CW]) for c in range(NCH)]
        rmax = sb("rmax", [P, 8, 4])
        shifted = sb("shifted", [P, 3, 512])
        probs = sb("probs", [P, 2, QUADS, 512])
        inverse = sb("inverse", [P, 2, 128])

        scores = [ps(f"scores{i}") for i in range(3)]
        turned = [ps(f"turned{i}") for i in range(2)]
        av = ps("av")
        dense = [ps(f"dense{i}") for i in range(2)]

        x_loaded = sem("x_loaded")
        ctx_loaded = sem("ctx_loaded")
        small_loaded = sem("small_loaded")
        masks_loaded = sem("masks_loaded")
        wm_loaded = sem("wm_loaded")
        w_loaded = [sem(f"w_loaded{l}") for l in range(4)]
        stored = sem("stored")
        silu_ready = sem("silu_ready")
        masks_ready = sem("masks_ready")
        tables_summed = sem("tables_summed")
        setup_chain = sem("setup_chain")
        setup_done = sem("setup_done")
        vpad_zero = sem("vpad_zero")
        dense_full = [sem(f"dense_full{i}") for i in range(2)]
        dense_empty = [sem(f"dense_empty{i}") for i in range(2)]
        sq_ready = sem("sq_ready")
        lnv_ready = sem("lnv_ready")
        rstd_ready = sem("rstd_ready")
        xhat_ready = sem("xhat_ready")
        xn_ready = sem("xn_ready")
        rope_halves = sem("rope_halves")
        rope_summed = sem("rope_summed")
        qraw_ready = sem("qraw_ready")
        kraw_ready = sem("kraw_ready")
        q_ready = sem("q_ready")
        k_ready = sem("k_ready")
        v_ready = sem("v_ready")
        delta_ready = sem("delta_ready")
        x_ready = sem("x_ready")
        hidden_raw = sem("hidden_raw")
        hidden_ready = sem("hidden_ready")
        scores_ready = sem("scores_ready")
        max_ready = sem("max_ready")
        shifted_ready = sem("shifted_ready")
        turned_ready = sem("turned_ready")
        probs_ready = sem("probs_ready")
        av_ready = sem("av_ready")
        inverse_ready = sem("inverse_ready")
        out_ready = sem("out_ready")

        def wcol(key):
            return w[:, WCOL[key]:WCOL[key] + 128]

        def const(name):
            return cst[:, CCOL[name][0]:CCOL[name][1]]

        def tab(name):
            return {"cosq": cosq, "sinq": sinq}[name][:, :] if name in ("cosq", "sinq") else const(name)

        def chunk(name, c):
            if name == "x":
                return x[:, c * CW:(c + 1) * CW]
            if name == "ctx":
                return ctx[:, c * XW:(c + 1) * XW]
            return None

        def width_of(s):
            return XW if s["src"] == "ctx" else CW

        def wait_dense_full(eng, use):
            eng.wait_ge(dense_full[use % 2], use // 2 + 1)

        def post_bias(s):
            return {f"post{a}": a for a in range(NA)}.get(s["bias"], NA - 1 + int(s["bias"][-1]) if s["bias"][:3] == "mlp" else 0)

        def nk_of(n):
            return T if ATTN[n // PHASE_QUADS // NCH][1] else TC

        NQ = NE * PHASE_QUADS
        NU = NQ // QUADS

        block = stack.enter_context(nc.Block())

        @block.sync
        def _(sp):
            sp.dma_start(cst[:, :], consts).then_inc(small_loaded, 16)
            sp.dma_start(cond[:, :], condT).then_inc(small_loaded, 16)
            sp.dma_start(bm[:, :], bmod).then_inc(small_loaded, 16)
            sp.dma_start(nwt[:, :], nw).then_inc(small_loaded, 16)
            sp.dma_start(bc[:, :], bcols).then_inc(small_loaded, 16)
            sp.dma_start(m8[:, :], mask).then_inc(masks_loaded, 16)
            sp.dma_start(mT8[:, :], maskT).then_inc(masks_loaded, 16)
            sp.dma_start(cmT8[:, :], cmaskT).then_inc(masks_loaded, 16)
            sp.dma_start(cm8[:, :], cmask.to_broadcast([P, B * TC])).then_inc(masks_loaded, 16)
            sp.dma_start(x[:, :], xT).then_inc(x_loaded, 16)
            sp.dma_start(wm[:, :], wmod).then_inc(wm_loaded, 16)
            sp.dma_start(ctx[:, :], ctxT).then_inc(ctx_loaded, 16)
            for l in range(4):
                lo, hi = WSPAN[l]
                sp.dma_start(w[:, lo:hi], weights[:, lo:hi]).then_inc(w_loaded[l], 16)
            for c in range(NCH):
                sp.wait_ge(x_ready, last_posts[c])
                sp.dma_start(outT[:, c * CW:(c + 1) * CW], x[:, c * CW:(c + 1) * CW]).then_inc(stored, 16)
            sp.wait_ge(stored, 16 * NCH)

        @block.tensor
        def _(pe):
            def setup():
                pe.wait_ge(small_loaded, 5 * 16)
                pe.wait_ge(silu_ready, 1)
                pe.wait_ge(wm_loaded, 16)
                for t in range(2 * NM + NG):
                    name = (MODS + MODS + GATES)[t]
                    src = silu if name in MOD_OF_SILU else cond
                    pe.matmul(dense[0][:, B * t:B * t + B], wm[:, 128 * t:128 * t + 128], src[:, :], start=True, stop=True)
                first = (2 * NM + NG) * B
                pe.wait_ge(w_loaded[0], 16)
                pe.wait_ge(w_loaded[2], 16)
                for t, (key, bias) in enumerate([((0, "o"), "L0bv"), ((2, "so"), "L2bv"), ((2, "xo"), "L2bvc")]):
                    mm = pe.matmul(dense[0][:, first + t:first + t + 1], wcol(key), bc[:, BC[bias]:BC[bias] + 1], start=True, stop=True)
                mm.then_inc(tables_summed, 1)
                pe.wait_ge(masks_ready, 2)
                pe.matmul(dense[1][:, 0:T], const("ones"), mTf[:, :], start=True, stop=True)
                pe.matmul(dense[1][:, T:T + B], const("ones")[0:TC, :], cmTf[:, :], start=True, stop=True).then_inc(tables_summed, 1)

            def step(s):
                kind = s["kind"]
                if kind == "gelu":
                    return
                use, c = s["use"], s["c"]
                bank = dense[use % 2]
                if use >= 2:
                    pe.wait_ge(dense_empty[use % 2], use // 2)
                if kind == "center":
                    if s["src"] == "x":
                        pe.wait_ge(x_loaded, 16)
                        if s["x_posts"]:
                            pe.wait_ge(x_ready, s["x_posts"])
                    else:
                        pe.wait_ge(ctx_loaded, 16)
                    mm = pe.matmul(bank[:, 0:width_of(s)], const("center"), chunk(s["src"], c), start=True, stop=True)
                elif kind == "var":
                    pe.wait_ge(sq_ready, s["norm"] + 1)
                    mm = pe.matmul(bank[:, 0:width_of(s)], const("mean"), sq[:, 0:width_of(s)], start=True, stop=True)
                elif kind == "proj":
                    pe.wait_ge(w_loaded[s["w"][0]], 16)
                    if s["src"] == "xn":
                        pe.wait_ge(xn_ready, s["norm"])
                    src = chunk("ctx", c) if s["src"] == "ctx" else xn[:, 0:s["width"]]
                    mm = pe.matmul(bank[:, 0:s["width"]], wcol(s["w"]), src, start=True, stop=True)
                elif kind == "v":
                    if s["src"] == "xn":
                        pe.wait_ge(xn_ready, s["norm"])
                    n = s["n"]
                    src = chunk("ctx", c) if s["src"] == "ctx" else xn[:, 0:CB * n]
                    for b in range(CB):
                        mm = pe.matmul(bank[0:n, 128 * b:128 * b + 128], src[:, n * b:n * b + n], wcol(s["w"]), start=True, stop=True)
                elif kind == "post":
                    pe.wait_ge(out_ready, CB * (s["phase"] - NCH + 1))
                    mm = pe.matmul(bank[:, :], wcol(s["w"]), oT[c][:, :], start=True, stop=True)
                elif kind == "up":
                    pe.wait_ge(xn_ready, s["norm"])
                    mm = pe.matmul(bank[:, :], wcol((s["layer"], f"up{s['j']}")), xn[:, :], start=True, stop=True)
                elif kind == "down":
                    pe.wait_ge(hidden_ready, s["mlp"] + 1)
                    for j in range(FF):
                        mm = pe.matmul(bank[:, :], wcol((s["layer"], f"dn{j}")), hid[:, j, :], start=(j == 0), stop=(j == FF - 1))
                mm.then_inc(dense_full[use % 2], 1)

            def score(n):
                e, g, b = n // PHASE_QUADS, n % QUADS, n // QUADS % CB
                c, nk = e % NCH, nk_of(n)
                layer, own = ATTN[e // NCH]
                if n % PHASE_QUADS == 0:
                    pe.wait_ge(q_ready, e + 1)
                    pe.wait_ge(k_ready, e + 1)
                if n >= 3:
                    pe.wait_ge(shifted_ready, n - 2)
                out = scores[n % 3][:, 0:4 * nk].rearrange("p (h k) -> p h k", h=4)
                masked = layer == 1
                mm = pe.matmul(out, qz[c][:, g, T * b:T * b + T], kbd[c][:, :, nk * b:nk * b + nk], start=True, stop=not masked)
                if masked and own:
                    mm = pe.matmul(out, identb[:, :], mb[:, None, :].to_broadcast([P, 4, T]), start=False, stop=True)
                elif masked:
                    bb = c * CB + b
                    mm = pe.matmul(out, identb[:, :], cb[:, bb:bb + 1, :].to_broadcast([P, 4, TC]), start=False, stop=True)
                mm.then_inc(scores_ready, 1)

            def turn(n):
                nk = nk_of(n)
                pe.wait_ge(shifted_ready, n + 1)
                if n >= 2:
                    pe.wait_ge(probs_ready, n - 1)
                for i in range(4):
                    mm = pe.transpose(turned[n % 2][0:nk, 128 * i:128 * i + 128], shifted[:, n % 3, nk * i:nk * i + nk], const("ident"))
                mm.then_inc(turned_ready, 1)

            def weigh(u):
                e, b = u // CB, u % CB
                c, nk = e % NCH, nk_of(u * QUADS)
                pe.wait_ge(probs_ready, QUADS * (u + 1))
                if b == 0:
                    pe.wait_ge(v_ready, e + 1)
                if u >= 1:
                    pe.wait_ge(out_ready, u)
                for i in range(4):
                    for g in range(QUADS):
                        pe.matmul(av[32 * g:32 * g + 32, 0:128], vpad[c][0:nk, b, g, i, :], probs[0:nk, u % 2, g, 128 * i:128 * i + 128],
                                  start=(i == 0), stop=(i == 3), skip_group_check=True)
                for i in range(4):
                    for g in range(QUADS):
                        mm = pe.matmul(av[32 * g:32 * g + 32, 128:256], const("headones")[0:nk, 32 * i:32 * i + 32],
                                       probs[0:nk, u % 2, g, 128 * i:128 * i + 128], start=(i == 0), stop=(i == 3), skip_group_check=True)
                mm.then_inc(av_ready, 1)

            setup()
            pe.wait_ge(setup_done, 1)
            for slot in lists[0]:
                for s in slot:
                    step(s)
            for e in range(NE):
                first = e * PHASE_QUADS
                for n in range(first, first + 3):
                    score(n)
                for j in range(PHASE_QUADS):
                    n = first + j
                    turn(n)
                    if j + 3 < PHASE_QUADS:
                        score(n + 3)
                    if n % QUADS == 1 and n > QUADS:
                        weigh(n // QUADS - 1)
                    for s in lists[e + 1][j]:
                        step(s)
            weigh(NU - 1)
            for slot in lists[NE + 1]:
                for s in slot:
                    step(s)

        @block.scalar
        def _(act):
            def step(s):
                kind, c = s["kind"], s["c"]
                if kind == "gelu":
                    act.wait_ge(hidden_raw, FF * (s["mlp"] + 1))
                    func = ACT.Gelu if s["layer"] == 3 else ACT.Gelu_apprx_tanh
                    act.activation(hid[:, :, :], hid[:, :, :], func).then_inc(hidden_ready, 1)
                    act.preload_act_table_set(EXP_LN_SET)
                    return
                if s.get("mode") in ("rope", "rope2", "any"):
                    return
                use = s["use"]
                bank = dense[use % 2]
                wait_dense_full(act, use)
                if kind == "center":
                    wd = width_of(s)
                    if s["norm"]:
                        act.wait_ge(xn_ready, s["norm"])
                    act.activation(sq[:, 0:wd], bank[:, 0:wd], ACT.Square).then_inc(sq_ready, 1)
                    act.activation(xc[:, 0:wd], bank[:, 0:wd], ACT.Copy).then_inc(dense_empty[use % 2], 1)
                elif kind == "var":
                    wd = width_of(s)
                    eps = epst[:, 1:2] if s["eps"] == 1e-6 else epst[:, 0:1]
                    act.activation(lnv[:, 0:wd], bank[:, 0:wd], ACT.Ln, bias=eps).then_inc(dense_empty[use % 2], 1)
                    act.wait_ge(dense_empty[use % 2], use // 2 + 1)
                    act.activation(rstd[:, 0:wd], lnv[:, 0:wd], ACT.Exp, scale=-0.5).then_inc(rstd_ready, 1)
                elif kind == "proj":
                    wd = s["width"]
                    bias = bc[:, BC[s["bias"]]:BC[s["bias"]] + 1]
                    dst = qraw if s["dst"] == "q" else kraw
                    if s["phase"]:
                        act.wait_ge(q_ready if s["dst"] == "q" else k_ready, s["phase"])
                    act.activation(dst[:, 0:wd], bank[:, 0:wd], ACT.Identity, bias=bias).then_inc(dense_empty[use % 2], 1)
                    act.wait_ge(dense_empty[use % 2], use // 2 + 1)
                    act.sem_inc(qraw_ready if s["dst"] == "q" else kraw_ready, 1)
                elif kind == "v":
                    n = s["n"]
                    if s["phase"] < NCH:
                        act.wait_ge(vpad_zero, s["phase"] + 1)
                    rows = vpad[c][0:n, :, :, :, :].rearrange("p b g i r -> p (b g) (i r)")
                    dst = diagonal(rows)
                    src = bank[0:n, :].rearrange("p (a i d) -> p a i d", i=4, d=HD)
                    act.activation(dst, src, ACT.Copy).then_inc(dense_empty[use % 2], 1)
                    act.wait_ge(dense_empty[use % 2], use // 2 + 1)
                    act.sem_inc(v_ready, 1)
                elif kind in ("post", "down"):
                    if s["post"]:
                        act.wait_ge(x_ready, s["post"])
                    col = post_bias(s)
                    if s["gate"] is None:
                        ins = act.activation(delta[:, :], bank[:, :], ACT.Identity, bias=pbias[:, col, 0:1])
                    else:
                        row = 2 * NM + GATES.index(s["gate"])
                        for b in range(CB):
                            bb = c * CB + b
                            ins = act.activation(delta[:, T * b:T * b + T], bank[:, T * b:T * b + T], ACT.Identity,
                                                 bias=pbias[:, col, bb:bb + 1], scale=mod[:, row, bb:bb + 1])
                    ins.then_inc(dense_empty[use % 2], 1)
                    act.wait_ge(dense_empty[use % 2], use // 2 + 1)
                    act.sem_inc(delta_ready, 1)
                elif kind == "up":
                    b1 = BC[f"L{s['layer']}b1_{s['j']}"]
                    act.activation(hid[:, s["j"], :], bank[:, :], ACT.Identity, bias=bc[:, b1:b1 + 1]).then_inc(dense_empty[use % 2], 1)
                    act.wait_ge(dense_empty[use % 2], use // 2 + 1)
                    act.sem_inc(hidden_raw, 1)

            def diagonal(rows):
                ap = rows[:, :, 0:4 * (32 + HD) - 32].copy() if hasattr(rows, "copy") else rows
                return bass.AP(tensor=rows.tensor, offset=rows.offset, ap=[list(rows.ap[0]), list(rows.ap[1]), [32 + HD, 4], [1, HD]])

            def exps(n):
                nk, u = nk_of(n), n // QUADS
                act.wait_ge(turned_ready, n + 1)
                if n % QUADS == 0 and u >= 2:
                    act.wait_ge(av_ready, u - 1)
                act.activation(probs[0:nk, u % 2, n % QUADS, :], turned[n % 2][0:nk, :], ACT.Exp, scale=SCALE).then_inc(probs_ready, 1)

            act.wait_ge(small_loaded, 5 * 16)
            act.activation(silu[:, :], cond[:, :], ACT.Silu).then_inc(silu_ready, 1)
            act.preload_act_table_set(EXP_LN_SET)
            act.wait_ge(setup_done, 1)
            for slot in lists[0]:
                for s in slot:
                    step(s)
            for e in range(NE):
                for j in range(PHASE_QUADS):
                    n = e * PHASE_QUADS + j
                    exps(n)
                    for s in lists[e + 1][j]:
                        step(s)
            for slot in lists[NE + 1]:
                for s in slot:
                    step(s)

        @block.vector
        def _(dve):
            linked = [0]

            def link(ins):
                linked[0] += 1
                ins.then_inc(setup_chain, 1)
                dve.wait_ge(setup_chain, linked[0])

            def setup():
                dve.memset(epst[:, 0:1], 1e-5)
                link(dve.memset(epst[:, 1:2], 1e-6))
                link(dve.memset(onesb[:, :], 1.0))
                link(dve.memset(pbias[:, :, :], 0.0))
                dve.wait_ge(masks_loaded, 4 * 16)
                dve.tensor_copy(mTf[:, :], mT8[:, :]).then_inc(masks_ready, 1)
                dve.tensor_copy(cmTf[:, :], cmT8[:, :]).then_inc(masks_ready, 1)
                dve.tensor_copy(mf[:, :], m8[:, :])
                link(dve.tensor_copy(cmf[:, :, :], cm8[:, :].rearrange("p (b k) -> p b k", b=B)))
                dve.wait_ge(small_loaded, 5 * 16)
                link(dve.tensor_copy(identb[:, :], const("ident")))
                link(dve.tensor_reduce(anyr[:, :], mf[:, :], AX_X, ALU.max))
                link(dve.tensor_scalar(noany[:, :], anyr[:, :], -1.0, 1.0, ALU.mult, ALU.add))
                link(dve.tensor_scalar(mf[:, :], mf[:, :], noany[:, 0:1], -1.0, ALU.max, ALU.add))
                link(dve.tensor_scalar(mb[:, :], mf[:, :], BIG, None, ALU.mult))
                dve.wait_ge(tables_summed, 2)
                link(dve.tensor_scalar(anyq[:, :], dense[1][:, 0:T], 1.0, None, ALU.min))
                link(dve.tensor_scalar(anyc[:, :], dense[1][:, T:T + B], 1.0, None, ALU.min))
                dve.tensor_tensor(cosq[:, :], const("cos2"), anyq[:, :], ALU.mult)
                link(dve.tensor_tensor(sinq[:, :], const("sin2"), anyq[:, :], ALU.mult))
                link(dve.tensor_scalar(noanyc[:, :], anyc[:, :], -1.0, 1.0, ALU.mult, ALU.add))
                link(dve.tensor_tensor(cmf[:, :, :], cmf[:, :, :], noanyc[:, :, None].to_broadcast([P, B, TC]), ALU.max))
                link(dve.tensor_scalar(cb[:, :, :], cmf[:, :, :], -1.0, BIG, ALU.add, ALU.mult))
                nt = 2 * NM + NG
                link(dve.tensor_tensor(mod[:, :, :], dense[0][:, 0:nt * B].rearrange("p (t b) -> p t b", b=B),
                                       bm[:, :, None].to_broadcast([P, nt, B]), ALU.add))
                link(dve.scalar_tensor_tensor(out=mod[:, 0:NM, :], in0=mod[:, 0:NM, :], scalar=1.0,
                                              in1=nwt[:, :, None].to_broadcast([P, NM, B]), op0=ALU.add, op1=ALU.mult))
                for t, bias in enumerate(["L0bp", "L2bproj", "L2bcp"]):
                    link(dve.tensor_tensor(pcol[:, t:t + 1], dense[0][:, nt * B + t:nt * B + t + 1], bc[:, BC[bias]:BC[bias] + 1], ALU.add))

                def gated(col, gate, bias):
                    if gate is None:
                        link(dve.tensor_copy(pbias[:, col, 0:1], bias))
                    else:
                        row = 2 * NM + GATES.index(gate)
                        link(dve.tensor_scalar(pbias[:, col, :], mod[:, row, :], bias, None, ALU.mult))

                gated(0, None, pcol[:, 0:1])
                gated(3, "L2a", pcol[:, 1:2])
                gated(4, None, pcol[:, 2:3])
                gated(NA - 1 + 1, "L1m", bc[:, BC["L1b2"]:BC["L1b2"] + 1])
                gated(NA - 1 + 2, "L2m", bc[:, BC["L2b2"]:BC["L2b2"] + 1])
                gated(NA - 1 + 3, None, bc[:, BC["L3b2"]:BC["L3b2"] + 1])
                dve.memset(rmax[:, :, :], 0.0).then_inc(setup_done, 1)

            def step(s):
                if s.get("mode") not in ("rope", "rope2", "any"):
                    return
                use, c, mode = s["use"], s["c"], s["mode"]
                bank = dense[use % 2]
                wait_dense_full(dve, use)
                if mode == "any":
                    dve.wait_ge(q_ready, s["phase"])
                    dve.tensor_tensor(qraw[:, :].rearrange("p (b t) -> p b t", b=CB), bank[:, :].rearrange("p (b t) -> p b t", b=CB),
                                      anyc[:, c * CB:(c + 1) * CB, None].to_broadcast([P, CB, T]), ALU.mult).then_inc(dense_empty[use % 2], 1)
                    dve.wait_ge(dense_empty[use % 2], use // 2 + 1)
                    dve.sem_inc(qraw_ready, 1)
                    return
                wd, period = s["width"], s["period"]
                if mode == "rope" and s["rope"]:
                    dve.wait_ge(rope_summed, s["rope"])
                dst = ropea if mode == "rope" else ropeb
                t = tab(s["tabs"][mode == "rope2"])[:, 0:period]
                dve.tensor_tensor(dst[:, 0:wd].rearrange("p (b t) -> p b t", t=period), bank[:, 0:wd].rearrange("p (b t) -> p b t", t=period),
                                  t[:, None, :].to_broadcast([P, CB, period]), ALU.mult).then_inc(dense_empty[use % 2], 1)
                dve.wait_ge(dense_empty[use % 2], use // 2 + 1)
                dve.sem_inc(rope_halves, 1)

            def row_max(n):
                nk = nk_of(n)
                dve.wait_ge(scores_ready, n + 1)
                dve.tensor_reduce(rmax[:, n % 8, :], scores[n % 3][:, 0:4 * nk].rearrange("p (h k) -> p h k", h=4),
                                  AX_X, ALU.max).then_inc(max_ready, 1)

            def shift(n):
                nk = nk_of(n)
                dve.wait_ge(max_ready, n + 1)
                if n >= 3:
                    dve.wait_ge(turned_ready, n - 2)
                dve.tensor_tensor(shifted[:, n % 3, 0:4 * nk].rearrange("p (h k) -> p h k", h=4),
                                  scores[n % 3][:, 0:4 * nk].rearrange("p (h k) -> p h k", h=4),
                                  rmax[:, n % 8, :, None].to_broadcast([P, 4, nk]), ALU.subtract).then_inc(shifted_ready, 1)

            def invert(u):
                dve.wait_ge(av_ready, u + 1)
                dve.reciprocal(inverse[:, u % 2, :], av[:, 128:256]).then_inc(inverse_ready, 1)

            def divide(u):
                e, b = u // CB, u % CB
                dve.wait_ge(inverse_ready, u + 1)
                dve.tensor_tensor(oT[e % NCH][:, T * b:T * b + T], av[:, 0:128], inverse[:, u % 2, :], ALU.mult).then_inc(out_ready, 1)

            setup()
            for slot in lists[0]:
                for s in slot:
                    step(s)
            for e in range(NE):
                first = e * PHASE_QUADS
                row_max(first)
                for j in range(PHASE_QUADS):
                    n = first + j
                    if j + 1 < PHASE_QUADS:
                        row_max(n + 1)
                    shift(n)
                    if n % QUADS == 2 and n > QUADS:
                        invert(n // QUADS - 1)
                    if n % QUADS == 3 and n > QUADS:
                        divide(n // QUADS - 1)
                    for s in lists[e + 1][j]:
                        step(s)
            invert(NU - 1)
            divide(NU - 1)
            for slot in lists[NE + 1]:
                for s in slot:
                    step(s)

        @block.gpsimd
        def _(pool):
            def step(s):
                kind, c = s["kind"], s["c"]
                if kind == "var":
                    wd = width_of(s)
                    per = wd // CB
                    pool.wait_ge(rstd_ready, s["norm"] + 1)
                    if s["xn_reader"] >= 0:
                        wait_dense_full(pool, s["xn_reader"])
                    if s["mod"] is None:
                        pool.tensor_tensor(xn[:, 0:wd], xc[:, 0:wd], rstd[:, 0:wd], ALU.mult).then_inc(xn_ready, 1)
                        pool.sem_inc(xhat_ready, 1)
                        return
                    pool.tensor_tensor(xhat[:, 0:wd], xc[:, 0:wd], rstd[:, 0:wd], ALU.mult).then_inc(xhat_ready, 1)
                    pool.wait_ge(xhat_ready, s["norm"] + 1)
                    row = MODS.index(s["mod"])
                    for b in range(CB):
                        bb = c * CB + b
                        ins = pool.tensor_scalar(xn[:, per * b:per * b + per], xhat[:, per * b:per * b + per],
                                                 mod[:, row, bb:bb + 1], mod[:, NM + row, bb:bb + 1], ALU.mult, ALU.add)
                    ins.then_inc(xn_ready, 1)
                elif kind == "proj" and s["mode"] != "rope":
                    wd = s["width"]
                    isq = s["dst"] == "q"
                    raw = qraw if isq else kraw
                    if s["mode"] == "rope2":
                        pool.wait_ge(rope_halves, 2 * (s["rope"] + 1))
                        pool.tensor_tensor(raw[:, 0:wd], ropea[:, 0:wd], ropeb[:, 0:wd], ALU.add).then_inc(rope_summed, 1)
                        pool.wait_ge(rope_summed, s["rope"] + 1)
                    else:
                        pool.wait_ge(qraw_ready if isq else kraw_ready, s["raw"] + 1)
                    dst, masks = (qz[c], "groupmask") if isq else (kbd[c], "headmask")
                    for i in range(4):
                        ins = pool.tensor_scalar(dst[:, i, 0:wd], raw[:, 0:wd], const(masks)[:, i:i + 1], 1.0, ALU.mult, ALU.mult)
                    ins.then_inc(q_ready if isq else k_ready, 1)
                elif kind in ("post", "down"):
                    pool.wait_ge(delta_ready, s["post"] + 1)
                    xs = chunk("x", c)
                    pool.tensor_tensor(xs, xs, delta[:, :], ALU.add).then_inc(x_ready, 1)

            for c in range(NCH):
                pool.memset(vpad[c][:, :, :, :, :], 0.0).then_inc(vpad_zero, 1)
            pool.wait_ge(x_loaded, 16)
            pool.wait_ge(setup_done, 1)
            for slots in lists:
                for slot in slots:
                    for s in slot:
                        step(s)


def host_consts():
    p = np.arange(P)
    h, d = p // HD, p % HD
    inv = (1.0 / 10000.0 ** (np.arange(0, HD, 2, dtype=np.float32) / HD)).astype(np.float32)
    ang = (np.arange(T, dtype=np.float32)[None, :] * inv[d % 4][:, None]).astype(np.float32)
    cos, sin = np.cos(ang).astype(np.float32), np.sin(ang).astype(np.float32)
    sin = np.where((d < 4)[:, None], -sin, sin).astype(np.float32)
    half = T // 2
    headones = np.zeros((P, 4, 32), np.float32)
    for i in range(4):
        headones[:, i, HD * i:HD * i + HD] = 1.0
    parts = {
        "center": np.eye(P, dtype=np.float32) - np.float32(1.0 / D),
        "mean": np.full((P, P), 1.0 / D, np.float32),
        "ident": np.eye(P, dtype=np.float32),
        "ones": np.ones((P, P), np.float32),
        "headones": headones.reshape(P, 128),
        "headmask": (h[:, None] % 4 == np.arange(4)[None, :]).astype(np.float32),
        "groupmask": (h[:, None] // 4 == np.arange(4)[None, :]).astype(np.float32),
        "cos": cos, "sin": sin,
        "cos2": np.concatenate([cos[:, :half]] * 2, 1), "sin2": np.concatenate([sin[:, :half]] * 2, 1),
    }
    return np.concatenate([parts[n] for n in CONSTS], 1)


def kernel(**inputs):
    import concourse.bacc as bacc
    from concourse.bass_utils import run_bass_kernel_spmd

    g = {n: np.asarray(v) for n, v in inputs.items()}
    L0, L1, L2, L3 = ({n[9:]: v for n, v in g.items() if n.startswith(f"L{l}_xcond_")} for l in range(4))

    def cols(wt, i, size=128):
        return wt[:, size * i:size * i + size]

    def swapped(wt):
        return wt.reshape(wt.shape[0], H, 2, HD // 2)[:, :, ::-1, :].reshape(wt.shape[0], H * HD)

    aw, mw = L1["adaLN_W"], L2["W_mod"]
    ab, mb_ = L1["adaLN_b"].reshape(9, 128).T, L2["b_mod"].reshape(6, 128).T
    lw = {n: L3[f"ln{n}_w"].T for n in (1, 2, 3)}
    lb = {n: L3[f"ln{n}_b"].reshape(2, 128).T for n in (1, 2, 3)}

    def both(half):
        one, six = (1, 0)[half], (1, 0)[half]
        ws = [cols(L0["Wss_q"], half), cols(L0["Wss_kv"], half), cols(aw, one), cols(aw, 3 + one), cols(aw, 6 + one),
              cols(mw, six), cols(mw, 3 + six)] + [cols(lw[n], half) for n in (1, 2, 3)]
        bs = [L0["bss_q"].reshape(2, 128).T[:, half], L0["bss_kv"].reshape(2, 128).T[:, half], ab[:, one], ab[:, 3 + one], ab[:, 6 + one],
              mb_[:, six], mb_[:, 3 + six]] + [lb[n][:, half] for n in (1, 2, 3)]
        return ws, bs

    sw, sbias = both(0)
    hw, hbias = both(1)
    gw = [cols(aw, 2), cols(aw, 5), cols(aw, 8), cols(mw, 2), cols(mw, 5)]
    gbias = [ab[:, 2], ab[:, 5], ab[:, 8], mb_[:, 2], mb_[:, 5]]
    one = np.ones(128, np.float32)
    norm_w = [one, one, L1["norm1_w"], L1["normc_w"], L1["norm2_w"]] + [one] * 5

    def rope_qkv(wt, names):
        return {names[0]: cols(wt, 0), names[0] + "r": swapped(cols(wt, 0)), names[1]: cols(wt, 1), names[1] + "r": swapped(cols(wt, 1)), names[2]: cols(wt, 2)}

    def mlp(up, down):
        return {**{f"up{j}": cols(up, j) for j in range(FF)}, **{f"dn{j}": down[128 * j:128 * j + 128] for j in range(FF)}}

    wl = {
        0: dict(q=L0["Wq"], k=cols(L0["Wkv"], 0), v=cols(L0["Wkv"], 1), o=L0["Wp"]),
        1: dict(**rope_qkv(L1["qkv_W"], ("sq", "sk", "sv")), so=L1["attn_out_W"], xq=L1["cq_W"], xk=L1["ck_W"], xv=L1["cv_W"],
                xo=L1["co_W"], **mlp(L1["mlp_W1"], L1["mlp_W2"])),
        2: dict(sq=cols(L2["W_qkv"], 0), sk=cols(L2["W_qkv"], 1), sv=cols(L2["W_qkv"], 2), so=L2["W_proj"], xq=L2["W_qc"],
                xk=cols(L2["W_kvc"], 0), xv=cols(L2["W_kvc"], 1), xo=L2["W_cproj"], **mlp(L2["W_mlp1"], L2["W_mlp2"])),
        3: dict(**rope_qkv(L3["qkv_w"].T, ("sq", "sk", "sv")), so=L3["sa_out_w"].T, xq=L3["q_w"].T, xqr=swapped(L3["q_w"].T),
                xk=L3["k_w"].T, xkr=swapped(L3["k_w"].T), xv=L3["v_w"].T, xo=L3["ca_out_w"].T, **mlp(L3["ffn_w1"].T, L3["ffn_w2"].T)),
    }
    b_of = {"zero": np.zeros(128, np.float32), "L0bq": L0["bq"], "L0bk": L0["bkv"][:128], "L0bv": L0["bkv"][128:], "L0bp": L0["bp"],
            "L2bq": L2["b_qkv"][:128], "L2bk": L2["b_qkv"][128:256], "L2bv": L2["b_qkv"][256:], "L2bproj": L2["b_proj"],
            "L2bqc": L2["b_qc"], "L2bkc": L2["b_kvc"][:128], "L2bvc": L2["b_kvc"][128:], "L2bcp": L2["b_cproj"],
            "L1b2": L1["mlp_b2"], "L2b2": L2["b_mlp2"], "L3b2": L3["ffn_b2"]}
    for l, v in ((1, L1["mlp_b1"]), (2, L2["b_mlp1"]), (3, L3["ffn_b1"])):
        for j in range(FF):
            b_of[f"L{l}b1_{j}"] = v[128 * j:128 * j + 128]

    arrays = {
        "xT": g["x"].reshape(B * T, D).T,
        "ctxT": g["ctx_1024"].reshape(B * TC, D).T,
        "condT": g["cond_1024"].T,
        "wmod": np.concatenate(sw + hw + gw, 1),
        "bmod": np.stack(sbias + hbias + gbias, 1),
        "nw": np.stack(norm_w, 1),
        "weights": np.concatenate([wl[l][n] for l in WBLOCKS for n in WBLOCKS[l]], 1),
        "bcols": np.stack([b_of[n] for n in BCOLS], 1),
        "consts": host_consts(),
        "mask": g["mask_SxS_bk0"],
        "maskT": g["mask_SxS_bk0"].T,
        "cmaskT": g["mask_BxS2_bf1"].T,
        "cmask": g["mask_BxS2_bf1"].reshape(1, B * TC),
    }
    arrays = {n: np.ascontiguousarray(v) for n, v in arrays.items()}
    nc = bacc.Bacc("TRN2", target_bir_lowering=False, num_devices=1)
    args = [nc.dram_tensor(f"{n}_dram", v.shape, mybir.dt.from_np(v.dtype), kind="ExternalInput").ap() for n, v in arrays.items()]
    out = nc.dram_tensor("outT_dram", [D, B * T], F32, kind="ExternalOutput").ap()
    blocks_kernel(nc, *args, out)
    r = run_bass_kernel_spmd(nc, [{f"{n}_dram": v for n, v in arrays.items()}], core_ids=[0])
    return np.ascontiguousarray(r.results[0]["outT_dram"].T).reshape(B, T, D)
```

```python
from contextlib import ExitStack

import numpy as np

import concourse.bass as bass
from concourse import mybir

F32 = mybir.dt.float32
BF16 = mybir.dt.bfloat16
ALU = mybir.AluOpType
ACT = mybir.ActivationFunctionType
AX_X = mybir.AxisListType.X

P = 128
B, T, D = 8, 128, 128
TC = 77
H, HD = 16, 8
NCH = 2
CB = B // NCH
CW = CB * T
XW = CB * TC
FF = 4
SCALE = float(HD) ** -0.5
BIG = float(2.0 ** 100)
EXP_LN_SET = "natural_log_exp_and_others"

ATTN = [(0, False), (1, True), (1, False), (2, True), (2, False), (3, True), (3, False)]
NA = len(ATTN)
NE = NA * NCH
QUADS = 4
PHASE_QUADS = CB * QUADS

MODS = ["L0q", "L0kv", "L1sa", "L1x", "L1m", "L2a", "L2m", "L3n1", "L3n2", "L3n3"]
GATES = ["L1sa", "L1x", "L1m", "L2a", "L2m"]
NM, NG = len(MODS), len(GATES)
MOD_OF_SILU = ["L0q", "L0kv", "L2a", "L2m"]

BCOLS = ["zero", "L0bq", "L0bk", "L0bv", "L0bp", "L2bq", "L2bk", "L2bv", "L2bproj", "L2bqc", "L2bkc", "L2bvc", "L2bcp",
         "L1b2", "L2b2", "L3b2"] + [f"L{l}b1_{j}" for l in (1, 2, 3) for j in range(FF)]
BC = {n: i for i, n in enumerate(BCOLS)}
NBC = len(BCOLS)

WBLOCKS = {
    0: ["q", "k", "v", "o"],
    1: ["sq", "sqr", "sk", "skr", "sv", "so", "xq", "xk", "xv", "xo"] + [f"up{j}" for j in range(FF)] + [f"dn{j}" for j in range(FF)],
    2: ["sq", "sk", "sv", "so", "xq", "xk", "xv", "xo"] + [f"up{j}" for j in range(FF)] + [f"dn{j}" for j in range(FF)],
    3: ["sq", "sqr", "sk", "skr", "sv", "so", "xq", "xqr", "xk", "xkr", "xv", "xo"] + [f"up{j}" for j in range(FF)] + [f"dn{j}" for j in range(FF)],
}
WCOL = {}
for _l in WBLOCKS:
    for _n in WBLOCKS[_l]:
        WCOL[(_l, _n)] = 128 * len(WCOL)
NW = 128 * len(WCOL)
WSPAN = {l: (WCOL[(l, WBLOCKS[l][0])], WCOL[(l, WBLOCKS[l][-1])] + 128) for l in WBLOCKS}

CONSTS = {"center": 128, "mean": 128, "ident": 128, "ones": 128, "headones": 128, "headmask": 4, "groupmask": 4,
          "cos": 128, "sin": 128, "cos2": 128, "sin2": 128}
CCOL, NC = {}, 0
for _n, _w in CONSTS.items():
    CCOL[_n] = (NC, NC + _w)
    NC += _w


def dense_steps(f):
    a, c = divmod(f, NCH)
    steps = []

    def norm(src, mod, eps):
        steps.extend([dict(kind="center", src=src, c=c), dict(kind="var", src=src, mod=mod, eps=eps, c=c), None])

    def proj(dst, layer, name, mode, src="xn", width=CW, **more):
        steps.append(dict(kind="proj", dst=dst, w=(layer, name), mode=mode, src=src, width=width, c=c, **more))
        if mode == "rope":
            steps.append(dict(kind="proj", dst=dst, w=(layer, name + "r"), mode="rope2", src=src, width=width, c=c, **more))

    def post(a_done):
        layer, own = ATTN[a_done]
        gate = {(1, True): "L1sa", (1, False): "L1x", (2, True): "L2a"}.get((layer, own))
        w = (layer, "o" if layer == 0 else "so" if own else "xo")
        steps.append(dict(kind="post", w=w, gate=gate, bias={0: 0, 3: 1, 4: 2}.get(a_done, "zero"), c=c))

    def mlp(layer, mod, gate):
        norm("x", mod, 1e-6 if layer == 2 else 1e-5)
        steps.extend(dict(kind="up", layer=layer, j=j, c=c) for j in range(FF))
        steps.append(dict(kind="gelu", layer=layer, c=c))
        steps.append(dict(kind="down", layer=layer, gate=gate, bias=f"L{layer}b2", c=c))

    if a > 0:
        post(a - 1)
    if a == 3:
        mlp(1, "L1m", "L1m")
    if a == 5:
        mlp(2, "L2m", "L2m")
    if a == NA:
        mlp(3, "L3n3", None)
        return steps
    layer, own = ATTN[a]
    norm("x", {0: "L0q", 1: "L1sa", 2: "L1x", 3: "L2a", 4: None, 5: "L3n1", 6: "L3n2"}[a], 1e-6 if layer == 2 else 1e-5)
    if own:
        if layer == 2:
            proj("q", 2, "sq", "bias", bias="L2bq")
            proj("k", 2, "sk", "bias", bias="L2bk")
        else:
            tabs = ("cosq", "sinq", "cos2", "sin2") if layer == 1 else ("cos", "sin", "cos", "sin")
            proj("q", layer, "sq", "rope", tabs=tabs[0:2], period=T)
            proj("k", layer, "sk", "rope", tabs=tabs[2:4], period=T)
        steps.append(dict(kind="v", w=(layer, "sv"), src="xn", n=T, c=c))
    else:
        if layer == 0:
            proj("q", 0, "q", "bias", bias="L0bq")
            norm("ctx", "L0kv", 1e-5)
            proj("k", 0, "k", "bias", bias="L0bk", width=XW)
        elif layer == 1:
            proj("q", 1, "xq", "any")
            proj("k", 1, "xk", "bias", src="ctx", bias="zero", width=XW)
        elif layer == 2:
            proj("q", 2, "xq", "bias", bias="L2bqc")
            norm("ctx", None, 1e-6)
            proj("k", 2, "xk", "bias", bias="L2bkc", width=XW)
        else:
            proj("q", 3, "xq", "rope", tabs=("cos", "sin"), period=T)
            proj("k", 3, "xk", "rope", src="ctx", tabs=("cos", "sin"), width=XW, period=TC)
        src = "xn" if layer in (0, 2) else "ctx"
        steps.append(dict(kind="v", w=(layer, "v" if layer == 0 else "xv"), src=src, n=TC, c=c))
    return steps


INV = 1
FIRST_SLOT, LAST_SLOT = 2, 12


def plan():
    count = dict(use=0, norm=0, rope=0, qraw=0, kraw=0, post=0, mlp=0, up=0)
    posts = [0] * NCH
    lists = []
    xn_reader = -1
    for f in range(NE + NCH):
        steps = dense_steps(f)
        slots = [[] for _ in range(PHASE_QUADS)]
        for at, s in enumerate(steps):
            if s is None:
                continue
            slots[FIRST_SLOT + at * (LAST_SLOT + 1 - FIRST_SLOT) // len(steps)].append(s)
            s["phase"] = f
            kind = s["kind"]
            if kind != "gelu":
                s["use"] = count["use"]
                count["use"] += 1
            s["norm"] = count["norm"] - (kind == "var")
            s["xn_reader"] = xn_reader
            if kind == "center":
                count["norm"] += 1
                s["x_posts"] = count["post"]
            if kind == "up" or s.get("src") == "xn":
                xn_reader = s["use"]
            if s.get("mode") in ("rope", "rope2"):
                s["rope"] = count["rope"]
                count["rope"] += s["mode"] == "rope2"
            if kind == "proj" and s["mode"] in ("bias", "any"):
                s["raw"] = count[s["dst"] + "raw"]
                count[s["dst"] + "raw"] += 1
            if kind in ("post", "down"):
                s["post"] = count["post"]
                count["post"] += 1
                posts[s["c"]] = count["post"]
            s["mlp"] = count["mlp"]
            count["mlp"] += kind == "down"
        lists.append(slots)
    return lists, posts


def blocks_kernel(nc, xT, ctxT, condT, wmod, bmod, nw, weights, bcols, consts, mask, maskT, cmaskT, cmask, outT):
    lists, last_posts = plan()
    with ExitStack() as stack:
        def sb(name, shape, dt=F32):
            return stack.enter_context(nc.sbuf_tensor(name, shape, dt))

        def ps(name):
            return stack.enter_context(nc.psum_tensor(name, [P, 512], F32))

        def sem(name):
            return stack.enter_context(nc.semaphore(name))

        x = sb("x", [P, B * T])
        ctx = sb("ctx", [P, B * TC])
        cond = sb("cond", [P, B])
        wm = sb("wm", [P, (2 * NM + NG) * 128])
        bm = sb("bm", [P, 2 * NM + NG])
        nwt = sb("nwt", [P, NM])
        w = sb("w", [P, NW])
        bc = sb("bc", [P, NBC])
        cst = sb("cst", [P, NC])
        m8 = sb("m8", [P, T], mybir.dt.uint8)
        mT8 = sb("mT8", [P, T], mybir.dt.uint8)
        cmT8 = sb("cmT8", [TC, B], mybir.dt.uint8)
        cm8 = sb("cm8", [P, B * TC], mybir.dt.uint8)
        silu = sb("silu", [P, B])
        mod = sb("mod", [P, 2 * NM + NG, B])
        pcol = sb("pcol", [P, 3])
        epst = sb("epst", [P, 2])
        mf = sb("mf", [P, T])
        mTf = sb("mTf", [P, T])
        cmTf = sb("cmTf", [TC, B])
        cmf = sb("cmf", [P, B, TC])
        anyq = sb("anyq", [P, T])
        cosq = sb("cosq", [P, T])
        sinq = sb("sinq", [P, T])
        anyc = sb("anyc", [P, B])
        noanyc = sb("noanyc", [P, B])
        anyr = sb("anyr", [P, 1])
        noany = sb("noany", [P, 1])
        mb = sb("mb", [P, T], BF16)
        cb = sb("cb", [P, B, TC], BF16)
        identb = sb("identb", [P, 128], BF16)
        onesb = sb("onesb", [P, 128], BF16)
        sq = sb("sq", [P, CW])
        lnv = sb("lnv", [P, CW])
        rstd = sb("rstd", [P, CW])
        xhat = sb("xhat", [P, CW])
        xn = sb("xn", [P, CW])
        ropea = sb("ropea", [P, CW])
        ropeb = sb("ropeb", [P, CW])
        qraw = sb("qraw", [P, CW])
        kraw = sb("kraw", [P, CW])
        delta = sb("delta", [P, CW])
        hid = sb("hid", [P, FF, CW])
        qz = [sb(f"qz{c}", [P, QUADS, CW]) for c in range(NCH)]
        kbd = [sb(f"kbd{c}", [P, 4, CW]) for c in range(NCH)]
        vpad = [sb(f"vpad{c}", [P, CB, 4, 4, 32]) for c in range(NCH)]
        oT = [sb(f"oT{c}", [P, CW]) for c in range(NCH)]
        rmax = sb("rmax", [P, 8, 4])
        shifted = sb("shifted", [P, 3, 512])
        probs = sb("probs", [P, 2, QUADS, 512])
        inverse = sb("inverse", [P, 2, 128])

        scores = [ps(f"scores{i}") for i in range(3)]
        turned = [ps(f"turned{i}") for i in range(2)]
        av = ps("av")
        dense = [ps(f"dense{i}") for i in range(2)]

        x_loaded = sem("x_loaded")
        ctx_loaded = sem("ctx_loaded")
        small_loaded = sem("small_loaded")
        masks_loaded = sem("masks_loaded")
        wm_loaded = sem("wm_loaded")
        w_loaded = [sem(f"w_loaded{l}") for l in range(4)]
        stored = sem("stored")
        silu_ready = sem("silu_ready")
        masks_ready = sem("masks_ready")
        tables_summed = sem("tables_summed")
        setup_chain = sem("setup_chain")
        setup_done = sem("setup_done")
        vpad_zero = sem("vpad_zero")
        dense_full = [sem(f"dense_full{i}") for i in range(2)]
        dense_empty = [sem(f"dense_empty{i}") for i in range(2)]
        sq_ready = sem("sq_ready")
        lnv_ready = sem("lnv_ready")
        rstd_ready = sem("rstd_ready")
        xhat_ready = sem("xhat_ready")
        xn_ready = sem("xn_ready")
        rope_halves = sem("rope_halves")
        rope_summed = sem("rope_summed")
        qraw_ready = sem("qraw_ready")
        kraw_ready = sem("kraw_ready")
        q_ready = sem("q_ready")
        k_ready = sem("k_ready")
        v_ready = sem("v_ready")
        
        x_ready = sem("x_ready")
        hidden_raw = sem("hidden_raw")
        hidden_ready = sem("hidden_ready")
        scores_ready = sem("scores_ready")
        max_ready = sem("max_ready")
        shifted_ready = sem("shifted_ready")
        turned_ready = sem("turned_ready")
        probs_ready = sem("probs_ready")
        av_ready = sem("av_ready")
        inverse_ready = sem("inverse_ready")
        out_ready = sem("out_ready")

        def wcol(key):
            return w[:, WCOL[key]:WCOL[key] + 128]

        def const(name):
            return cst[:, CCOL[name][0]:CCOL[name][1]]

        def tab(name):
            return {"cosq": cosq, "sinq": sinq}[name][:, :] if name in ("cosq", "sinq") else const(name)

        def chunk(name, c):
            if name == "x":
                return x[:, c * CW:(c + 1) * CW]
            if name == "ctx":
                return ctx[:, c * XW:(c + 1) * XW]
            return None

        def width_of(s):
            return XW if s["src"] == "ctx" else CW

        def wait_dense_full(eng, use):
            eng.wait_ge(dense_full[use % 2], use // 2 + 1)

        def post_bias(s):
            return pcol[:, s["bias"]:s["bias"] + 1] if isinstance(s["bias"], int) else bc[:, BC[s["bias"]]:BC[s["bias"]] + 1]

        def nk_of(n):
            return T if ATTN[n // PHASE_QUADS // NCH][1] else TC

        NQ = NE * PHASE_QUADS
        NU = NQ // QUADS

        block = stack.enter_context(nc.Block())

        @block.sync
        def _(sp):
            sp.dma_start(cst[:, :], consts).then_inc(small_loaded, 16)
            sp.dma_start(cond[:, :], condT).then_inc(small_loaded, 16)
            sp.dma_start(bm[:, :], bmod).then_inc(small_loaded, 16)
            sp.dma_start(nwt[:, :], nw).then_inc(small_loaded, 16)
            sp.dma_start(bc[:, :], bcols).then_inc(small_loaded, 16)
            sp.dma_start(m8[:, :], mask).then_inc(masks_loaded, 16)
            sp.dma_start(mT8[:, :], maskT).then_inc(masks_loaded, 16)
            sp.dma_start(cmT8[:, :], cmaskT).then_inc(masks_loaded, 16)
            sp.dma_start(cm8[:, :], cmask.to_broadcast([P, B * TC])).then_inc(masks_loaded, 16)
            sp.dma_start(x[:, :], xT).then_inc(x_loaded, 16)
            sp.dma_start(wm[:, :], wmod).then_inc(wm_loaded, 16)
            sp.dma_start(ctx[:, :], ctxT).then_inc(ctx_loaded, 16)
            for l in range(4):
                lo, hi = WSPAN[l]
                sp.dma_start(w[:, lo:hi], weights[:, lo:hi]).then_inc(w_loaded[l], 16)
            for c in range(NCH):
                sp.wait_ge(x_ready, last_posts[c])
                sp.dma_start(outT[:, c * CW:(c + 1) * CW], x[:, c * CW:(c + 1) * CW]).then_inc(stored, 16)
            sp.wait_ge(stored, 16 * NCH)

        @block.tensor
        def _(pe):
            def setup():
                pe.wait_ge(small_loaded, 5 * 16)
                pe.wait_ge(silu_ready, 1)
                pe.wait_ge(wm_loaded, 16)
                for t in range(2 * NM + NG):
                    name = (MODS + MODS + GATES)[t]
                    src = silu if name in MOD_OF_SILU else cond
                    pe.matmul(dense[0][:, B * t:B * t + B], wm[:, 128 * t:128 * t + 128], src[:, :], start=True, stop=True)
                first = (2 * NM + NG) * B
                pe.wait_ge(w_loaded[0], 16)
                pe.wait_ge(w_loaded[2], 16)
                for t, (key, bias) in enumerate([((0, "o"), "L0bv"), ((2, "so"), "L2bv"), ((2, "xo"), "L2bvc")]):
                    mm = pe.matmul(dense[0][:, first + t:first + t + 1], wcol(key), bc[:, BC[bias]:BC[bias] + 1], start=True, stop=True)
                mm.then_inc(tables_summed, 1)
                pe.wait_ge(masks_ready, 2)
                pe.matmul(dense[1][:, 0:T], const("ones"), mTf[:, :], start=True, stop=True)
                pe.matmul(dense[1][:, T:T + B], const("ones")[0:TC, :], cmTf[:, :], start=True, stop=True).then_inc(tables_summed, 1)

            def step(s):
                kind = s["kind"]
                if kind == "gelu":
                    return
                use, c = s["use"], s["c"]
                bank = dense[use % 2]
                if use >= 2:
                    pe.wait_ge(dense_empty[use % 2], use // 2)
                if kind == "center":
                    if s["src"] == "x":
                        pe.wait_ge(x_loaded, 16)
                        if s["x_posts"]:
                            pe.wait_ge(x_ready, s["x_posts"])
                    else:
                        pe.wait_ge(ctx_loaded, 16)
                    mm = pe.matmul(bank[:, 0:width_of(s)], const("center"), chunk(s["src"], c), start=True, stop=True)
                elif kind == "var":
                    pe.wait_ge(sq_ready, s["norm"] + 1)
                    mm = pe.matmul(bank[:, 0:width_of(s)], const("mean"), sq[:, 0:width_of(s)], start=True, stop=True)
                elif kind == "proj":
                    pe.wait_ge(w_loaded[s["w"][0]], 16)
                    if s["src"] == "xn":
                        pe.wait_ge(xn_ready, s["norm"])
                    src = chunk("ctx", c) if s["src"] == "ctx" else xn[:, 0:s["width"]]
                    mm = pe.matmul(bank[:, 0:s["width"]], wcol(s["w"]), src, start=True, stop=True)
                elif kind == "v":
                    if s["src"] == "xn":
                        pe.wait_ge(xn_ready, s["norm"])
                    n = s["n"]
                    src = chunk("ctx", c) if s["src"] == "ctx" else xn[:, 0:CB * n]
                    for b in range(CB):
                        mm = pe.matmul(bank[0:n, 128 * b:128 * b + 128], src[:, n * b:n * b + n], wcol(s["w"]), start=True, stop=True)
                elif kind == "post":
                    pe.wait_ge(out_ready, CB * (s["phase"] - NCH + 1))
                    mm = pe.matmul(bank[:, :], wcol(s["w"]), oT[c][:, :], start=True, stop=True)
                elif kind == "up":
                    pe.wait_ge(xn_ready, s["norm"])
                    mm = pe.matmul(bank[:, :], wcol((s["layer"], f"up{s['j']}")), xn[:, :], start=True, stop=True)
                elif kind == "down":
                    pe.wait_ge(hidden_ready, s["mlp"] + 1)
                    for j in range(FF):
                        mm = pe.matmul(bank[:, :], wcol((s["layer"], f"dn{j}")), hid[:, j, :], start=(j == 0), stop=(j == FF - 1))
                mm.then_inc(dense_full[use % 2], 1)

            def score(n):
                e, g, b = n // PHASE_QUADS, n % QUADS, n // QUADS % CB
                c, nk = e % NCH, nk_of(n)
                layer, own = ATTN[e // NCH]
                if g == 0:
                    pe.wait_ge(q_ready, n // QUADS + 1)
                    pe.wait_ge(k_ready, n // QUADS + 1)
                if n >= 3:
                    pe.wait_ge(shifted_ready, n - 2)
                out = scores[n % 3][:, 0:4 * nk].rearrange("p (h k) -> p h k", h=4)
                masked = layer == 1
                mm = pe.matmul(out, qz[c][:, g, T * b:T * b + T], kbd[c][:, :, nk * b:nk * b + nk], start=True, stop=not masked)
                if masked and own:
                    mm = pe.matmul(out, identb[:, :], mb[:, None, :].to_broadcast([P, 4, T]), start=False, stop=True)
                elif masked:
                    bb = c * CB + b
                    mm = pe.matmul(out, identb[:, :], cb[:, bb:bb + 1, :].to_broadcast([P, 4, TC]), start=False, stop=True)
                mm.then_inc(scores_ready, 1)

            def turn(n):
                nk = nk_of(n)
                pe.wait_ge(shifted_ready, n + 1)
                if n >= 2:
                    pe.wait_ge(probs_ready, n - 1)
                for i in range(4):
                    mm = pe.transpose(turned[n % 2][0:nk, 128 * i:128 * i + 128], shifted[:, n % 3, nk * i:nk * i + nk], const("ident"))
                mm.then_inc(turned_ready, 1)

            def weigh(u):
                e, b = u // CB, u % CB
                c, nk = e % NCH, nk_of(u * QUADS)
                pe.wait_ge(probs_ready, QUADS * (u + 1))
                if b == 0:
                    pe.wait_ge(v_ready, e + 1)
                if u >= 1:
                    pe.wait_ge(out_ready, u)
                for i in range(4):
                    for g in range(QUADS):
                        pe.matmul(av[32 * g:32 * g + 32, 0:128], vpad[c][0:nk, b, g, i, :], probs[0:nk, u % 2, g, 128 * i:128 * i + 128],
                                  start=(i == 0), stop=(i == 3), skip_group_check=True)
                for i in range(4):
                    for g in range(QUADS):
                        mm = pe.matmul(av[32 * g:32 * g + 32, 128:256], const("headones")[0:nk, 32 * i:32 * i + 32],
                                       probs[0:nk, u % 2, g, 128 * i:128 * i + 128], start=(i == 0), stop=(i == 3), skip_group_check=True)
                mm.then_inc(av_ready, 1)

            setup()
            pe.wait_ge(setup_done, 1)
            for slot in lists[0]:
                for s in slot:
                    step(s)
            for n in range(3):
                score(n)
            for e in range(NE):
                for j in range(PHASE_QUADS):
                    n = e * PHASE_QUADS + j
                    turn(n)
                    if n + 3 < NQ:
                        score(n + 3)
                    for s in lists[e + 1][j]:
                        step(s)
                    if n % QUADS == 0 and n:
                        weigh(n // QUADS - 1)
            weigh(NU - 1)
            for slot in lists[NE + 1]:
                for s in slot:
                    step(s)

        @block.scalar
        def _(act):
            def step(s):
                kind, c = s["kind"], s["c"]
                if kind == "gelu":
                    act.wait_ge(hidden_raw, FF * (s["mlp"] + 1))
                    func = ACT.Gelu if s["layer"] == 3 else ACT.Gelu_apprx_tanh
                    act.activation(hid[:, :, :], hid[:, :, :], func).then_inc(hidden_ready, 1)
                    act.preload_act_table_set(EXP_LN_SET)
                    return
                if s.get("mode") in ("rope", "rope2", "any") or kind in ("post", "down"):
                    return
                use = s["use"]
                bank = dense[use % 2]
                wait_dense_full(act, use)
                if kind == "center":
                    wd = width_of(s)
                    act.activation(sq[:, 0:wd], bank[:, 0:wd], ACT.Square).then_inc(sq_ready, 1)
                elif kind == "var":
                    wd = width_of(s)
                    eps = epst[:, 1:2] if s["eps"] == 1e-6 else epst[:, 0:1]
                    act.activation(lnv[:, 0:wd], bank[:, 0:wd], ACT.Ln, bias=eps).then_inc(dense_empty[use % 2], 1)
                    act.wait_ge(dense_empty[use % 2], use // 2 + 1)
                    if s["norm"]:
                        act.wait_ge(xhat_ready, s["norm"])
                    act.activation(rstd[:, 0:wd], lnv[:, 0:wd], ACT.Exp, scale=-0.5).then_inc(rstd_ready, 1)
                elif kind == "proj":
                    wd = s["width"]
                    bias = bc[:, BC[s["bias"]]:BC[s["bias"]] + 1]
                    dst = qraw if s["dst"] == "q" else kraw
                    if s["phase"]:
                        act.wait_ge(q_ready if s["dst"] == "q" else k_ready, CB * s["phase"])
                    act.activation(dst[:, 0:wd], bank[:, 0:wd], ACT.Identity, bias=bias).then_inc(dense_empty[use % 2], 1)
                    act.wait_ge(dense_empty[use % 2], use // 2 + 1)
                    act.sem_inc(qraw_ready if s["dst"] == "q" else kraw_ready, 1)
                elif kind == "v":
                    n = s["n"]
                    if s["phase"] < NCH:
                        act.wait_ge(vpad_zero, s["phase"] + 1)
                    rows = vpad[c][0:n, :, :, :, :].rearrange("p b g i r -> p (b g) (i r)")
                    dst = diagonal(rows)
                    src = bank[0:n, :].rearrange("p (a i d) -> p a i d", i=4, d=HD)
                    act.activation(dst, src, ACT.Copy).then_inc(dense_empty[use % 2], 1)
                    act.wait_ge(dense_empty[use % 2], use // 2 + 1)
                    act.sem_inc(v_ready, 1)
                elif kind == "up":
                    b1 = BC[f"L{s['layer']}b1_{s['j']}"]
                    act.activation(hid[:, s["j"], :], bank[:, :], ACT.Identity, bias=bc[:, b1:b1 + 1]).then_inc(dense_empty[use % 2], 1)
                    act.wait_ge(dense_empty[use % 2], use // 2 + 1)
                    act.sem_inc(hidden_raw, 1)

            def diagonal(rows):
                ap = rows[:, :, 0:4 * (32 + HD) - 32].copy() if hasattr(rows, "copy") else rows
                return bass.AP(tensor=rows.tensor, offset=rows.offset, ap=[list(rows.ap[0]), list(rows.ap[1]), [32 + HD, 4], [1, HD]])

            def exps(n):
                nk, u = nk_of(n), n // QUADS
                act.wait_ge(turned_ready, n + 1)
                if n % QUADS == 0 and u >= 2:
                    act.wait_ge(av_ready, u - 1)
                act.activation(probs[0:nk, u % 2, n % QUADS, :], turned[n % 2][0:nk, :], ACT.Exp, scale=SCALE).then_inc(probs_ready, 1)

            act.wait_ge(small_loaded, 5 * 16)
            act.activation(silu[:, :], cond[:, :], ACT.Silu).then_inc(silu_ready, 1)
            act.preload_act_table_set(EXP_LN_SET)
            act.wait_ge(setup_done, 1)
            for slot in lists[0]:
                for s in slot:
                    step(s)
            for e in range(NE):
                for j in range(PHASE_QUADS):
                    n = e * PHASE_QUADS + j
                    exps(n)
                    for s in lists[e + 1][j]:
                        step(s)
            for slot in lists[NE + 1]:
                for s in slot:
                    step(s)

        @block.vector
        def _(dve):
            linked = [0]

            def link(ins):
                linked[0] += 1
                ins.then_inc(setup_chain, 1)
                dve.wait_ge(setup_chain, linked[0])

            def setup():
                dve.memset(epst[:, 0:1], 1e-5)
                link(dve.memset(epst[:, 1:2], 1e-6))
                link(dve.memset(onesb[:, :], 1.0))
                dve.wait_ge(masks_loaded, 4 * 16)
                dve.tensor_copy(mTf[:, :], mT8[:, :]).then_inc(masks_ready, 1)
                dve.tensor_copy(cmTf[:, :], cmT8[:, :]).then_inc(masks_ready, 1)
                dve.tensor_copy(mf[:, :], m8[:, :])
                link(dve.tensor_copy(cmf[:, :, :], cm8[:, :].rearrange("p (b k) -> p b k", b=B)))
                dve.wait_ge(small_loaded, 5 * 16)
                link(dve.tensor_copy(identb[:, :], const("ident")))
                link(dve.tensor_reduce(anyr[:, :], mf[:, :], AX_X, ALU.max))
                link(dve.tensor_scalar(noany[:, :], anyr[:, :], -1.0, 1.0, ALU.mult, ALU.add))
                link(dve.tensor_scalar(mf[:, :], mf[:, :], noany[:, 0:1], -1.0, ALU.max, ALU.add))
                link(dve.tensor_scalar(mb[:, :], mf[:, :], BIG, None, ALU.mult))
                dve.wait_ge(tables_summed, 2)
                link(dve.tensor_scalar(anyq[:, :], dense[1][:, 0:T], 1.0, None, ALU.min))
                link(dve.tensor_scalar(anyc[:, :], dense[1][:, T:T + B], 1.0, None, ALU.min))
                dve.tensor_tensor(cosq[:, :], const("cos2"), anyq[:, :], ALU.mult)
                link(dve.tensor_tensor(sinq[:, :], const("sin2"), anyq[:, :], ALU.mult))
                link(dve.tensor_scalar(noanyc[:, :], anyc[:, :], -1.0, 1.0, ALU.mult, ALU.add))
                link(dve.tensor_tensor(cmf[:, :, :], cmf[:, :, :], noanyc[:, :, None].to_broadcast([P, B, TC]), ALU.max))
                link(dve.tensor_scalar(cb[:, :, :], cmf[:, :, :], -1.0, BIG, ALU.add, ALU.mult))
                nt = 2 * NM + NG
                link(dve.tensor_tensor(mod[:, :, :], dense[0][:, 0:nt * B].rearrange("p (t b) -> p t b", b=B),
                                       bm[:, :, None].to_broadcast([P, nt, B]), ALU.add))
                link(dve.scalar_tensor_tensor(out=mod[:, 0:NM, :], in0=mod[:, 0:NM, :], scalar=1.0,
                                              in1=nwt[:, :, None].to_broadcast([P, NM, B]), op0=ALU.add, op1=ALU.mult))
                for t, bias in enumerate(["L0bp", "L2bproj", "L2bcp"]):
                    link(dve.tensor_tensor(pcol[:, t:t + 1], dense[0][:, nt * B + t:nt * B + t + 1], bc[:, BC[bias]:BC[bias] + 1], ALU.add))

                dve.memset(rmax[:, :, :], 0.0).then_inc(setup_done, 1)

            def spread(dst, raw, mask, nt, ready):
                for b in range(CB):
                    dve.tensor_tensor(dst[:, :, nt * b:nt * b + nt], raw[:, None, nt * b:nt * b + nt].to_broadcast([P, 4, nt]),
                                      mask[:, :, None].to_broadcast([P, 4, nt]), ALU.mult).then_inc(ready, 1)

            def step(s):
                kind, c, mode = s["kind"], s["c"], s.get("mode")
                if kind == "var":
                    wd = width_of(s)
                    per = wd // CB
                    use = s["use"] - 1
                    dve.wait_ge(rstd_ready, s["norm"] + 1)
                    if s["xn_reader"] >= 0:
                        wait_dense_full(dve, s["xn_reader"])
                    plain = s["mod"] is None
                    dst = xn if plain else xhat
                    dve.tensor_tensor(dst[:, 0:wd], dense[use % 2][:, 0:wd], rstd[:, 0:wd], ALU.mult).then_inc(dense_empty[use % 2], 1)
                    dve.wait_ge(dense_empty[use % 2], use // 2 + 1)
                    dve.sem_inc(xhat_ready, 1)
                    if plain:
                        dve.sem_inc(xn_ready, 1)
                        return
                    row = MODS.index(s["mod"])
                    for b in range(CB):
                        bb = c * CB + b
                        ins = dve.tensor_scalar(xn[:, per * b:per * b + per], xhat[:, per * b:per * b + per],
                                                mod[:, row, bb:bb + 1], mod[:, NM + row, bb:bb + 1], ALU.mult, ALU.add)
                    ins.then_inc(xn_ready, 1)
                    return
                if kind in ("post", "down"):
                    use = s["use"]
                    bank, xs = dense[use % 2], chunk("x", c)
                    wait_dense_full(dve, use)
                    if s["gate"] is None:
                        dve.scalar_tensor_tensor(out=xs, in0=bank[:, :], scalar=post_bias(s), in1=xs, op0=ALU.add, op1=ALU.add)\
                           .then_inc(dense_empty[use % 2], 1)
                        dve.wait_ge(dense_empty[use % 2], use // 2 + 1)
                        dve.sem_inc(x_ready, 1)
                        return
                    gates = mod[:, 2 * NM + GATES.index(s["gate"]), c * CB:(c + 1) * CB, None].to_broadcast([P, CB, T])
                    dve.scalar_tensor_tensor(out=delta[:, :].rearrange("p (b t) -> p b t", b=CB), in0=bank[:, :].rearrange("p (b t) -> p b t", b=CB),
                                             scalar=post_bias(s), in1=gates, op0=ALU.add, op1=ALU.mult).then_inc(dense_empty[use % 2], 1)
                    dve.wait_ge(dense_empty[use % 2], use // 2 + 1)
                    dve.tensor_tensor(xs, xs, delta[:, :], ALU.add).then_inc(x_ready, 1)
                    return
                if kind != "proj":
                    return
                if s["dst"] == "k" and mode == "bias":
                    dve.wait_ge(kraw_ready, s["raw"] + 1)
                    spread(kbd[c], kraw, const("headmask"), s["width"] // CB, k_ready)
                if mode == "bias":
                    return
                use = s["use"]
                bank = dense[use % 2]
                wait_dense_full(dve, use)
                if mode == "any":
                    dve.wait_ge(q_ready, CB * s["phase"])
                    dve.tensor_tensor(qraw[:, :].rearrange("p (b t) -> p b t", b=CB), bank[:, :].rearrange("p (b t) -> p b t", b=CB),
                                      anyc[:, c * CB:(c + 1) * CB, None].to_broadcast([P, CB, T]), ALU.mult).then_inc(dense_empty[use % 2], 1)
                    dve.wait_ge(dense_empty[use % 2], use // 2 + 1)
                    dve.sem_inc(qraw_ready, 1)
                    return
                wd, period = s["width"], s["period"]
                if mode == "rope" and s["rope"]:
                    dve.wait_ge(rope_summed, s["rope"])
                dst = ropea if mode == "rope" else ropeb
                t = tab(s["tabs"][mode == "rope2"])[:, 0:period]
                dve.tensor_tensor(dst[:, 0:wd].rearrange("p (b t) -> p b t", t=period), bank[:, 0:wd].rearrange("p (b t) -> p b t", t=period),
                                  t[:, None, :].to_broadcast([P, CB, period]), ALU.mult).then_inc(dense_empty[use % 2], 1)
                dve.wait_ge(dense_empty[use % 2], use // 2 + 1)
                dve.sem_inc(rope_halves, 1)
                if mode == "rope2" and s["dst"] == "k":
                    if s["phase"]:
                        dve.wait_ge(k_ready, CB * s["phase"])
                    dve.tensor_tensor(kraw[:, 0:wd], ropea[:, 0:wd], ropeb[:, 0:wd], ALU.add).then_inc(rope_summed, 1)
                    dve.wait_ge(rope_summed, s["rope"] + 1)
                    spread(kbd[c], kraw, const("headmask"), period, k_ready)

            def row_max(n):
                nk = nk_of(n)
                dve.wait_ge(scores_ready, n + 1)
                dve.tensor_reduce(rmax[:, n % 8, :], scores[n % 3][:, 0:4 * nk].rearrange("p (h k) -> p h k", h=4),
                                  AX_X, ALU.max).then_inc(max_ready, 1)

            def shift(n):
                nk = nk_of(n)
                dve.wait_ge(max_ready, n + 1)
                if n >= 3:
                    dve.wait_ge(turned_ready, n - 2)
                dve.tensor_tensor(shifted[:, n % 3, 0:4 * nk].rearrange("p (h k) -> p h k", h=4),
                                  scores[n % 3][:, 0:4 * nk].rearrange("p (h k) -> p h k", h=4),
                                  rmax[:, n % 8, :, None].to_broadcast([P, 4, nk]), ALU.subtract).then_inc(shifted_ready, 1)

            def invert(u):
                dve.wait_ge(av_ready, u + 1)
                dve.reciprocal(inverse[:, u % 2, :], av[:, 128:256]).then_inc(inverse_ready, 1)

            def divide(u):
                e, b = u // CB, u % CB
                dve.wait_ge(inverse_ready, u + 1)
                dve.tensor_tensor(oT[e % NCH][:, T * b:T * b + T], av[:, 0:128], inverse[:, u % 2, :], ALU.mult).then_inc(out_ready, 1)

            setup()
            for slot in lists[0]:
                for s in slot:
                    step(s)
            row_max(0)
            row_max(1)
            shift(0)
            for e in range(NE):
                for j in range(PHASE_QUADS):
                    n = e * PHASE_QUADS + j
                    if n + 2 < NQ:
                        row_max(n + 2)
                    if n + 1 < NQ:
                        shift(n + 1)
                    if n:
                        for s in lists[(n - 1) // PHASE_QUADS + 1][(n - 1) % PHASE_QUADS]:
                            step(s)
                    if n % QUADS == INV and n > QUADS:
                        invert(n // QUADS - 1)
                        divide(n // QUADS - 1)
            for s in lists[NE][PHASE_QUADS - 1]:
                step(s)
            invert(NU - 1)
            divide(NU - 1)
            for slot in lists[NE + 1]:
                for s in slot:
                    step(s)

        @block.gpsimd
        def _(pool):
            def step(s):
                if s["kind"] != "proj" or s["dst"] != "q" or s["mode"] == "rope":
                    return
                c = s["c"]
                if s["mode"] == "rope2":
                    pool.wait_ge(rope_halves, 2 * (s["rope"] + 1))
                    if s["phase"]:
                        pool.wait_ge(q_ready, CB * s["phase"])
                    pool.tensor_tensor(qraw[:, :], ropea[:, :], ropeb[:, :], ALU.add).then_inc(rope_summed, 1)
                    pool.wait_ge(rope_summed, s["rope"] + 1)
                else:
                    pool.wait_ge(qraw_ready, s["raw"] + 1)
                for b in range(CB):
                    pool.tensor_tensor(qz[c][:, :, T * b:T * b + T], qraw[:, None, T * b:T * b + T].to_broadcast([P, QUADS, T]),
                                       const("groupmask")[:, :, None].to_broadcast([P, QUADS, T]), ALU.mult).then_inc(q_ready, 1)

            for c in range(NCH):
                pool.memset(vpad[c][:, :, :, :, :], 0.0).then_inc(vpad_zero, 1)
            pool.wait_ge(x_loaded, 16)
            pool.wait_ge(setup_done, 1)
            for slots in lists:
                for slot in slots:
                    for s in slot:
                        step(s)


def host_consts():
    p = np.arange(P)
    h, d = p // HD, p % HD
    inv = (1.0 / 10000.0 ** (np.arange(0, HD, 2, dtype=np.float32) / HD)).astype(np.float32)
    ang = (np.arange(T, dtype=np.float32)[None, :] * inv[d % 4][:, None]).astype(np.float32)
    cos, sin = np.cos(ang).astype(np.float32), np.sin(ang).astype(np.float32)
    sin = np.where((d < 4)[:, None], -sin, sin).astype(np.float32)
    half = T // 2
    headones = np.zeros((P, 4, 32), np.float32)
    for i in range(4):
        headones[:, i, HD * i:HD * i + HD] = 1.0
    parts = {
        "center": np.eye(P, dtype=np.float32) - np.float32(1.0 / D),
        "mean": np.full((P, P), 1.0 / D, np.float32),
        "ident": np.eye(P, dtype=np.float32),
        "ones": np.ones((P, P), np.float32),
        "headones": headones.reshape(P, 128),
        "headmask": (h[:, None] % 4 == np.arange(4)[None, :]).astype(np.float32),
        "groupmask": (h[:, None] // 4 == np.arange(4)[None, :]).astype(np.float32),
        "cos": cos, "sin": sin,
        "cos2": np.concatenate([cos[:, :half]] * 2, 1), "sin2": np.concatenate([sin[:, :half]] * 2, 1),
    }
    return np.concatenate([parts[n] for n in CONSTS], 1)


def kernel(**inputs):
    import concourse.bacc as bacc
    from concourse.bass_utils import run_bass_kernel_spmd

    g = {n: np.asarray(v) for n, v in inputs.items()}
    L0, L1, L2, L3 = ({n[9:]: v for n, v in g.items() if n.startswith(f"L{l}_xcond_")} for l in range(4))

    def cols(wt, i, size=128):
        return wt[:, size * i:size * i + size]

    def swapped(wt):
        return wt.reshape(wt.shape[0], H, 2, HD // 2)[:, :, ::-1, :].reshape(wt.shape[0], H * HD)

    aw, mw = L1["adaLN_W"], L2["W_mod"]
    ab, mb_ = L1["adaLN_b"].reshape(9, 128).T, L2["b_mod"].reshape(6, 128).T
    lw = {n: L3[f"ln{n}_w"].T for n in (1, 2, 3)}
    lb = {n: L3[f"ln{n}_b"].reshape(2, 128).T for n in (1, 2, 3)}

    def both(half):
        one, six = (1, 0)[half], (1, 0)[half]
        ws = [cols(L0["Wss_q"], half), cols(L0["Wss_kv"], half), cols(aw, one), cols(aw, 3 + one), cols(aw, 6 + one),
              cols(mw, six), cols(mw, 3 + six)] + [cols(lw[n], half) for n in (1, 2, 3)]
        bs = [L0["bss_q"].reshape(2, 128).T[:, half], L0["bss_kv"].reshape(2, 128).T[:, half], ab[:, one], ab[:, 3 + one], ab[:, 6 + one],
              mb_[:, six], mb_[:, 3 + six]] + [lb[n][:, half] for n in (1, 2, 3)]
        return ws, bs

    sw, sbias = both(0)
    hw, hbias = both(1)
    gw = [cols(aw, 2), cols(aw, 5), cols(aw, 8), cols(mw, 2), cols(mw, 5)]
    gbias = [ab[:, 2], ab[:, 5], ab[:, 8], mb_[:, 2], mb_[:, 5]]
    one = np.ones(128, np.float32)
    norm_w = [one, one, L1["norm1_w"], L1["normc_w"], L1["norm2_w"]] + [one] * 5

    def rope_qkv(wt, names):
        return {names[0]: cols(wt, 0), names[0] + "r": swapped(cols(wt, 0)), names[1]: cols(wt, 1), names[1] + "r": swapped(cols(wt, 1)), names[2]: cols(wt, 2)}

    def mlp(up, down):
        return {**{f"up{j}": cols(up, j) for j in range(FF)}, **{f"dn{j}": down[128 * j:128 * j + 128] for j in range(FF)}}

    wl = {
        0: dict(q=L0["Wq"], k=cols(L0["Wkv"], 0), v=cols(L0["Wkv"], 1), o=L0["Wp"]),
        1: dict(**rope_qkv(L1["qkv_W"], ("sq", "sk", "sv")), so=L1["attn_out_W"], xq=L1["cq_W"], xk=L1["ck_W"], xv=L1["cv_W"],
                xo=L1["co_W"], **mlp(L1["mlp_W1"], L1["mlp_W2"])),
        2: dict(sq=cols(L2["W_qkv"], 0), sk=cols(L2["W_qkv"], 1), sv=cols(L2["W_qkv"], 2), so=L2["W_proj"], xq=L2["W_qc"],
                xk=cols(L2["W_kvc"], 0), xv=cols(L2["W_kvc"], 1), xo=L2["W_cproj"], **mlp(L2["W_mlp1"], L2["W_mlp2"])),
        3: dict(**rope_qkv(L3["qkv_w"].T, ("sq", "sk", "sv")), so=L3["sa_out_w"].T, xq=L3["q_w"].T, xqr=swapped(L3["q_w"].T),
                xk=L3["k_w"].T, xkr=swapped(L3["k_w"].T), xv=L3["v_w"].T, xo=L3["ca_out_w"].T, **mlp(L3["ffn_w1"].T, L3["ffn_w2"].T)),
    }
    b_of = {"zero": np.zeros(128, np.float32), "L0bq": L0["bq"], "L0bk": L0["bkv"][:128], "L0bv": L0["bkv"][128:], "L0bp": L0["bp"],
            "L2bq": L2["b_qkv"][:128], "L2bk": L2["b_qkv"][128:256], "L2bv": L2["b_qkv"][256:], "L2bproj": L2["b_proj"],
            "L2bqc": L2["b_qc"], "L2bkc": L2["b_kvc"][:128], "L2bvc": L2["b_kvc"][128:], "L2bcp": L2["b_cproj"],
            "L1b2": L1["mlp_b2"], "L2b2": L2["b_mlp2"], "L3b2": L3["ffn_b2"]}
    for l, v in ((1, L1["mlp_b1"]), (2, L2["b_mlp1"]), (3, L3["ffn_b1"])):
        for j in range(FF):
            b_of[f"L{l}b1_{j}"] = v[128 * j:128 * j + 128]

    arrays = {
        "xT": g["x"].reshape(B * T, D).T,
        "ctxT": g["ctx_1024"].reshape(B * TC, D).T,
        "condT": g["cond_1024"].T,
        "wmod": np.concatenate(sw + hw + gw, 1),
        "bmod": np.stack(sbias + hbias + gbias, 1),
        "nw": np.stack(norm_w, 1),
        "weights": np.concatenate([wl[l][n] for l in WBLOCKS for n in WBLOCKS[l]], 1),
        "bcols": np.stack([b_of[n] for n in BCOLS], 1),
        "consts": host_consts(),
        "mask": g["mask_SxS_bk0"],
        "maskT": g["mask_SxS_bk0"].T,
        "cmaskT": g["mask_BxS2_bf1"].T,
        "cmask": g["mask_BxS2_bf1"].reshape(1, B * TC),
    }
    arrays = {n: np.ascontiguousarray(v) for n, v in arrays.items()}
    nc = bacc.Bacc("TRN2", target_bir_lowering=False, num_devices=1)
    args = [nc.dram_tensor(f"{n}_dram", v.shape, mybir.dt.from_np(v.dtype), kind="ExternalInput").ap() for n, v in arrays.items()]
    out = nc.dram_tensor("outT_dram", [D, B * T], F32, kind="ExternalOutput").ap()
    blocks_kernel(nc, *args, out)
    r = run_bass_kernel_spmd(nc, [{f"{n}_dram": v for n, v in arrays.items()}], core_ids=[0])
    return np.ascontiguousarray(r.results[0]["outT_dram"].T).reshape(B, T, D)
```

```python
from contextlib import ExitStack

import numpy as np

import concourse.bass as bass
from concourse import mybir

F32 = mybir.dt.float32
BF16 = mybir.dt.bfloat16
ALU = mybir.AluOpType
ACT = mybir.ActivationFunctionType
AX_X = mybir.AxisListType.X

P = 128
B, T, D = 8, 128, 128
TC = 77
H, HD = 16, 8
NCH = 2
CB = B // NCH
CW = CB * T
HW = CW // 2
XW = CB * TC
FF = 4
SCALE = float(HD) ** -0.5
BIG = float(2.0 ** 100)
EXP_LN_SET = "natural_log_exp_and_others"
GELU_SET = "gelu_and_others"
GELU_TANH_SET = "gelu_apprx_tanh_and_others"

ATTN = [(0, False), (1, True), (1, False), (2, True), (2, False), (3, True), (3, False)]
NA = len(ATTN)
NE = NA * NCH
QUADS = 4
PHASE_QUADS = CB * QUADS

MODS = ["L0q", "L0kv", "L1sa", "L1x", "L1m", "L2a", "L2m", "L3n1", "L3n2", "L3n3"]
GATES = ["L1sa", "L1x", "L1m", "L2a", "L2m"]
NM, NG = len(MODS), len(GATES)
NM0 = 2
ROWS = ([("scale", n) for n in MODS[:NM0]] + [("shift", n) for n in MODS[:NM0]] + [("scale", n) for n in MODS[NM0:]]
        + [("shift", n) for n in MODS[NM0:]] + [("gate", n) for n in GATES])
ROW = {r: i for i, r in enumerate(ROWS)}
NR, NR0 = len(ROWS), 2 * NM0
MOD_OF_SILU = ["L0q", "L0kv", "L2a", "L2m"]

BCOLS = ["zero", "L0bq", "L0bk", "L0bv", "L0bp", "L2bq", "L2bk", "L2bv", "L2bproj", "L2bqc", "L2bkc", "L2bvc", "L2bcp",
         "L1b2", "L2b2", "L3b2"] + [f"L{l}b1_{j}" for l in (1, 2, 3) for j in range(FF)]
BC = {n: i for i, n in enumerate(BCOLS)}
NBC = len(BCOLS)

WBLOCKS = {
    0: ["q", "k", "v", "o"],
    1: ["sq", "sqr", "sk", "skr", "sv", "so", "xq", "xk", "xv", "xo"] + [f"up{j}" for j in range(FF)] + [f"dn{j}" for j in range(FF)],
    2: ["sq", "sk", "sv", "so", "xq", "xk", "xv", "xo"] + [f"up{j}" for j in range(FF)] + [f"dn{j}" for j in range(FF)],
    3: ["sq", "sqr", "sk", "skr", "sv", "so", "xq", "xqr", "xk", "xkr", "xv", "xo"] + [f"up{j}" for j in range(FF)] + [f"dn{j}" for j in range(FF)],
}
WCOL = {}
for _l in WBLOCKS:
    for _n in WBLOCKS[_l]:
        WCOL[(_l, _n)] = 128 * len(WCOL)
NW = 128 * len(WCOL)
WSPAN = {l: (WCOL[(l, WBLOCKS[l][0])], WCOL[(l, WBLOCKS[l][-1])] + 128) for l in WBLOCKS}

CONSTS = {"center": 128, "mean": 128, "headmask": 4, "groupscale": 4, "ident": 128, "ones": 128,
          "cos": 128, "sin": 128, "cos2": 128, "sin2": 128}
CCOL, NC = {}, 0
for _n, _w in CONSTS.items():
    CCOL[_n] = (NC, NC + _w)
    NC += _w
NC0 = CCOL["ident"][0]
NS = B + NR + NM - NM0 + NBC


def dense_steps(f):
    a, c = divmod(f, NCH)
    steps = []

    def norm(src, mod, eps):
        steps.extend([dict(kind="center", src=src, c=c), dict(kind="var", src=src, mod=mod, eps=eps, c=c)])

    def proj(dst, layer, name, mode, src="xn", width=CW, **more):
        steps.append(dict(kind="proj", dst=dst, w=(layer, name), mode=mode, src=src, width=width, c=c, **more))
        if mode == "rope":
            steps.append(dict(kind="proj", dst=dst, w=(layer, name + "r"), mode="rope2", src=src, width=width, c=c, **more))

    def post(a_done):
        layer, own = ATTN[a_done]
        gate = {(1, True): "L1sa", (1, False): "L1x", (2, True): "L2a"}.get((layer, own))
        w = (layer, "o" if layer == 0 else "so" if own else "xo")
        steps.append(dict(kind="post", w=w, gate=gate, bias={0: 0, 3: 1, 4: 2}.get(a_done, "zero"), c=c))

    def mlp(layer, mod, gate):
        norm("x", mod, 1e-6 if layer == 2 else 1e-5)
        steps.extend(dict(kind="up", layer=layer, j=j, c=c) for j in range(FF))
        steps.append(dict(kind="down", layer=layer, gate=gate, bias=f"L{layer}b2", c=c))

    def value(src, name, n):
        steps.append(dict(kind="v", w=(layer, name), src=src, n=n, c=c))

    layer, own = ATTN[a] if a < NA else (None, None)
    if layer == 0:
        norm("ctx", "L0kv", 1e-5)
        proj("k", 0, "k", "bias", bias="L0bk", width=XW)
        value("xn", "v", TC)
    elif layer is not None and not own:
        if layer == 1:
            proj("k", 1, "xk", "bias", src="ctx", bias="zero", width=XW)
        elif layer == 2:
            norm("ctx", None, 1e-6)
            proj("k", 2, "xk", "bias", bias="L2bkc", width=XW)
        else:
            proj("k", 3, "xk", "rope", src="ctx", tabs=("cos", "sin"), width=XW, period=TC)
        value("xn" if layer == 2 else "ctx", "xv", TC)
    if a > 0:
        post(a - 1)
    if a == 3:
        mlp(1, "L1m", "L1m")
    if a == 5:
        mlp(2, "L2m", "L2m")
    if a == NA:
        mlp(3, "L3n3", None)
        return steps
    norm("x", {0: "L0q", 1: "L1sa", 2: "L1x", 3: "L2a", 4: None, 5: "L3n1", 6: "L3n2"}[a], 1e-6 if layer == 2 else 1e-5)
    if not own:
        if layer == 0:
            proj("q", 0, "q", "bias", bias="L0bq")
        elif layer == 1:
            proj("q", 1, "xq", "any")
        elif layer == 2:
            proj("q", 2, "xq", "bias", bias="L2bqc")
        else:
            proj("q", 3, "xq", "rope", tabs=("cos", "sin"), period=T)
        return steps
    if layer == 2:
        proj("q", 2, "sq", "bias", bias="L2bq")
        proj("k", 2, "sk", "bias", bias="L2bk")
    else:
        tabs = ("cosq", "sinq", "cos2", "sin2") if layer == 1 else ("cos", "sin", "cos", "sin")
        proj("q", layer, "sq", "rope", tabs=tabs[0:2], period=T)
        proj("k", layer, "sk", "rope", tabs=tabs[2:4], period=T)
    value("xn", "sv", T)
    return steps


MODS_AFTER = {3: 2, 4: 4, 5: 9, 6: 6}
DIVIDE_SLOT = 1
SLOTS = {
    0: [3, 3, 5, 6, 7, 8, 10],
    1: [2, 3, 4, 6, 6, 11, 11, 11],
    2: [0, 3, 4, 7, 8, 10],
    3: [2, 3, 4, 6, 6, 6, 6, 7, 8, 8, 10, 11, 11],
    4: [0, 4, 6, 6, 6, 8, 11, 12],
    5: [2, 3, 4, 5, 5, 5, 5, 6, 7, 8, 9, 10, 11, 11, 11],
    6: [1, 3, 3, 4, 6, 7, 10, 10],
    7: [2, 3, 4, 6, 7, 7, 7, 14],
}


def plan():
    count = dict(use=0, norm=0, rope=0, qraw=0, kraw=0, post=0, mlp=0)
    posts = [0] * NCH
    lists = []
    xn_reader = -1
    for f in range(NE + 1):
        steps = dense_steps(f)
        slots = [[] for _ in range(PHASE_QUADS)]
        for s, at in zip(steps, SLOTS[f // NCH]):
            slots[at].append(s)
            s["phase"] = f
            kind = s["kind"]
            s["use"] = count["use"]
            count["use"] += 1
            s["norm"] = count["norm"] - (kind == "var")
            s["xn_reader"] = xn_reader
            if kind == "center":
                count["norm"] += 1
                s["x_posts"] = count["post"]
            if kind == "up" or s.get("src") == "xn":
                xn_reader = s["use"]
            if s.get("mode") in ("rope", "rope2"):
                s["rope"] = count["rope"]
                count["rope"] += s["mode"] == "rope2"
            if kind == "proj" and s["mode"] in ("bias", "any"):
                s["raw"] = count[s["dst"] + "raw"]
                count[s["dst"] + "raw"] += 1
            if kind in ("post", "down"):
                s["post"] = count["post"]
                count["post"] += 1
                posts[s["c"]] = count["post"]
            s["mlp"] = count["mlp"]
            count["mlp"] += kind == "down"
        lists.append(slots)
    return lists, posts, count["use"]


def blocks_kernel(nc, xT, ctxT, small, wmod, weights, consts, mask, maskT, cmaskT, cmask, outT):
    lists, posts, dense_uses = plan()
    with ExitStack() as stack:
        def sb(name, shape, dt=F32):
            return stack.enter_context(nc.sbuf_tensor(name, shape, dt))

        def ps(name):
            return stack.enter_context(nc.psum_tensor(name, [P, 512], F32))

        def sem(name):
            return stack.enter_context(nc.semaphore(name))

        x = sb("x", [P, B * T])
        ctx = sb("ctx", [P, B * TC])
        smalls = sb("smalls", [P, NS])
        cond, bm = smalls[:, 0:B], smalls[:, B:B + NR]
        nwt, bc = smalls[:, B + NR:NS - NBC], smalls[:, NS - NBC:NS]
        wm = sb("wm", [P, NR * 128])
        w = sb("w", [P, NW])
        cst = sb("cst", [P, NC])
        m8 = sb("m8", [P, T], mybir.dt.uint8)
        mT8 = sb("mT8", [P, T], mybir.dt.uint8)
        cmT8 = sb("cmT8", [TC, B], mybir.dt.uint8)
        cm8 = sb("cm8", [P, B * TC], mybir.dt.uint8)
        silu = sb("silu", [P, B])
        mod = sb("mod", [P, NR, B])
        pcol = sb("pcol", [P, 3])
        epst = sb("epst", [P, 2])
        mf = sb("mf", [P, T])
        mTf = sb("mTf", [P, T])
        cmTf = sb("cmTf", [TC, B])
        cmf = sb("cmf", [P, B, TC])
        anyq = sb("anyq", [P, T])
        cosq = sb("cosq", [P, T])
        sinq = sb("sinq", [P, T])
        anyc = sb("anyc", [P, B])
        noanyc = sb("noanyc", [P, B])
        anyr = sb("anyr", [P, 1])
        noany = sb("noany", [P, 1])
        mb = sb("mb", [P, T], BF16)
        cb = sb("cb", [P, B, TC], BF16)
        identb = sb("identb", [P, 128], BF16)
        sq = sb("sq", [P, CW])
        lnv = sb("lnv", [P, CW])
        rstd = sb("rstd", [P, CW])
        xhat = sb("xhat", [P, CW])
        xn = sb("xn", [P, CW])
        ropea = sb("ropea", [P, CW])
        ropeb = sb("ropeb", [P, CW])
        qraw = sb("qraw", [P, CW])
        kraw = sb("kraw", [P, CW])
        delta = sb("delta", [P, CW])
        hid = sb("hid", [P, FF, CW])
        qz = [sb(f"qz{c}", [P, QUADS, CW]) for c in range(NCH)]
        kbd = [sb(f"kbd{c}", [P, 4, CW]) for c in range(NCH)]
        vpad = [sb(f"vpad{c}", [P, CB, 4, 4, 32]) for c in range(NCH)]
        oT = [sb(f"oT{c}", [P, CW]) for c in range(NCH)]
        rmax = sb("rmax", [P, 8, 4])
        weights_q = sb("weights_q", [P, 3, 512])
        sums = sb("sums", [P, 2, H])
        inverse = sb("inverse", [P, H])
        inverse8 = sb("inverse8", [P, 2, P])
        probs = sb("probs", [P, 2, QUADS, 512])
        inverseT = sb("inverseT", [P, 128])

        scores = [ps(f"scores{i}") for i in range(3)]
        turned = [ps(f"turned{i}") for i in range(2)]
        av = ps("av")
        dense = [ps(f"dense{i}") for i in range(2)]

        x_loaded = [sem(f"x_loaded{c}") for c in range(NCH)]
        ctx_loaded = sem("ctx_loaded")
        small_loaded = sem("small_loaded")
        masks_loaded = sem("masks_loaded")
        wm_loaded = [sem(f"wm_loaded{i}") for i in range(2)]
        consts_loaded = [sem(f"consts_loaded{i}") for i in range(2)]
        w_loaded = [sem(f"w_loaded{l}") for l in range(4)]
        stored = sem("stored")
        silu_ready = sem("silu_ready")
        masks_ready = sem("masks_ready")
        eps_ready = sem("eps_ready")
        mod0_summed = sem("mod0_summed")
        mod0_ready = sem("mod0_ready")
        tables_summed = sem("tables_summed")
        setup_chain = sem("setup_chain")
        setup_done = sem("setup_done")
        vpad_zero = sem("vpad_zero")
        dense_full = [sem(f"dense_full{i}") for i in range(2)]
        dense_empty = [sem(f"dense_empty{i}") for i in range(2)]
        sq_ready = sem("sq_ready")
        rstd_ready = sem("rstd_ready")
        xhat_ready = sem("xhat_ready")
        xn_ready = sem("xn_ready")
        rope_halves = sem("rope_halves")
        rope_summed = sem("rope_summed")
        qraw_ready = sem("qraw_ready")
        kraw_ready = sem("kraw_ready")
        q_ready = sem("q_ready")
        k_ready = sem("k_ready")
        v_ready = sem("v_ready")
        x_ready = sem("x_ready")
        hidden_raw = sem("hidden_raw")
        hidden_ready = sem("hidden_ready")
        scores_ready = sem("scores_ready")
        max_ready = sem("max_ready")
        exp_ready = sem("exp_ready")
        turned_ready = sem("turned_ready")
        probs_ready = sem("probs_ready")
        av_ready = sem("av_ready")
        inverse_ready = sem("inverse_ready")
        inverse8_ready = sem("inverse8_ready")
        inverseT_ready = sem("inverseT_ready")
        out_ready = sem("out_ready")
        tail_full = sem("tail_full")
        tail_x = sem("tail_x")
        tail_sq = sem("tail_sq")
        tail_ln = sem("tail_ln")
        tail_rstd = sem("tail_rstd")
        tail_xhat = sem("tail_xhat")
        tail_xn = sem("tail_xn")
        tail_hidden = sem("tail_hidden")

        def wcol(key):
            return w[:, WCOL[key]:WCOL[key] + 128]

        def const(name):
            return cst[:, CCOL[name][0]:CCOL[name][1]]

        def tab(name):
            return {"cosq": cosq, "sinq": sinq}[name][:, :] if name in ("cosq", "sinq") else const(name)

        def chunk(name, c):
            if name == "x":
                return x[:, c * CW:(c + 1) * CW]
            if name == "ctx":
                return ctx[:, c * XW:(c + 1) * XW]
            return None

        def width_of(s):
            return XW if s["src"] == "ctx" else CW

        def wait_dense_full(eng, use):
            eng.wait_ge(dense_full[use % 2], use // 2 + 1)

        def post_bias(s):
            return pcol[:, s["bias"]:s["bias"] + 1] if isinstance(s["bias"], int) else bc[:, BC[s["bias"]]:BC[s["bias"]] + 1]

        def nk_of(n):
            return T if ATTN[n // PHASE_QUADS // NCH][1] else TC

        NQ = NE * PHASE_QUADS
        NU = NQ // QUADS

        tail_banks = scores + turned + dense

        def tail_bank(k):
            return tail_banks[k % len(tail_banks)][:, 0:HW]

        def half(t, h):
            return t[:, h * HW:(h + 1) * HW]

        def tail_input(h):
            return half(chunk("x", NCH - 1), h)

        USE_POST, USE_CENTER, USE_VAR, USE_UP, USE_DOWN = 0, 2, 4, 6, 6 + 2 * FF

        block = stack.enter_context(nc.Block())

        @block.sync
        def _(sp):
            def weights_of(l):
                lo, hi = WSPAN[l]
                sp.dma_start(w[:, lo:hi], weights[:, lo:hi]).then_inc(w_loaded[l], 16)

            sp.dma_start(smalls[:, :], small).then_inc(small_loaded, 16)
            sp.dma_start(cst[:, 0:NC0], consts[:, 0:NC0]).then_inc(consts_loaded[0], 16)
            sp.dma_start(ctx[:, :], ctxT).then_inc(ctx_loaded, 16)
            sp.dma_start(wm[:, 0:NR0 * 128], wmod[:, 0:NR0 * 128]).then_inc(wm_loaded[0], 16)
            weights_of(0)
            sp.dma_start(x[:, 0:CW], xT[:, 0:CW]).then_inc(x_loaded[0], 16)
            sp.dma_start(wm[:, NR0 * 128:NR * 128], wmod[:, NR0 * 128:NR * 128]).then_inc(wm_loaded[1], 16)
            sp.dma_start(cst[:, NC0:NC], consts[:, NC0:NC]).then_inc(consts_loaded[1], 16)
            sp.dma_start(x[:, CW:2 * CW], xT[:, CW:2 * CW]).then_inc(x_loaded[1], 16)
            sp.dma_start(m8[:, :], mask).then_inc(masks_loaded, 16)
            sp.dma_start(mT8[:, :], maskT).then_inc(masks_loaded, 16)
            sp.dma_start(cmT8[:, :], cmaskT).then_inc(masks_loaded, 16)
            sp.dma_start(cm8[:, :], cmask.to_broadcast([P, B * TC])).then_inc(masks_loaded, 16)
            for l in (2, 1, 3):
                weights_of(l)
            sp.wait_ge(x_ready, posts[0])
            sp.dma_start(outT[:, 0:CW], x[:, 0:CW]).then_inc(stored, 16)
            for h in range(2):
                lo, hi = CW + h * HW, CW + (h + 1) * HW
                sp.wait_ge(tail_x, 2 + h + 1)
                sp.dma_start(outT[:, lo:hi], x[:, lo:hi]).then_inc(stored, 16)
            sp.wait_ge(stored, 16 * 3)

        @block.tensor
        def _(pe):
            def modulations(rows):
                for t in rows:
                    src = silu[:, :] if ROWS[t][1] in MOD_OF_SILU else cond
                    mm = pe.matmul(av[:, B * t:B * t + B], wm[:, 128 * t:128 * t + 128], src, start=True, stop=True)
                return mm

            def setup_layer0():
                pe.wait_ge(small_loaded, 16)
                pe.wait_ge(silu_ready, 1)
                pe.wait_ge(wm_loaded[0], 16)
                modulations(range(NR0)).then_inc(mod0_summed, 1)

            def setup_rest():
                pe.wait_ge(w_loaded[2], 16)
                for t, (key, bias) in enumerate([((0, "o"), "L0bv"), ((2, "so"), "L2bv"), ((2, "xo"), "L2bvc")]):
                    pe.matmul(av[:, B * NR + t:B * NR + t + 1], wcol(key), bc[:, BC[bias]:BC[bias] + 1], start=True, stop=True)
                pe.wait_ge(masks_ready, 2)
                pe.matmul(av[:, 256:256 + T], const("ones"), mTf[:, :], start=True, stop=True)
                pe.matmul(av[:, 256 + T:256 + T + B], const("ones")[0:TC, :], cmTf[:, :], start=True, stop=True).then_inc(tables_summed, 1)

            def step(s):
                kind = s["kind"]
                use, c = s["use"], s["c"]
                bank = dense[use % 2]
                if use >= 2:
                    pe.wait_ge(dense_empty[use % 2], use // 2)
                if kind == "center":
                    pe.wait_ge(consts_loaded[0], 16)
                    if s["src"] == "x":
                        pe.wait_ge(x_loaded[c], 16)
                        if s["x_posts"]:
                            pe.wait_ge(x_ready, s["x_posts"])
                    else:
                        pe.wait_ge(ctx_loaded, 16)
                    mm = pe.matmul(bank[:, 0:width_of(s)], const("center"), chunk(s["src"], c), start=True, stop=True)
                elif kind == "var":
                    pe.wait_ge(sq_ready, s["norm"] + 1)
                    mm = pe.matmul(bank[:, 0:width_of(s)], const("mean"), sq[:, 0:width_of(s)], start=True, stop=True)
                elif kind == "proj":
                    pe.wait_ge(w_loaded[s["w"][0]], 16)
                    if s["src"] == "xn":
                        pe.wait_ge(xn_ready, s["norm"])
                    src = chunk("ctx", c) if s["src"] == "ctx" else xn[:, 0:s["width"]]
                    mm = pe.matmul(bank[:, 0:s["width"]], wcol(s["w"]), src, start=True, stop=True)
                elif kind == "v":
                    if s["src"] == "xn":
                        pe.wait_ge(xn_ready, s["norm"])
                    n = s["n"]
                    src = chunk("ctx", c) if s["src"] == "ctx" else xn[:, 0:CB * n]
                    for b in range(CB):
                        mm = pe.matmul(bank[0:n, 128 * b:128 * b + 128], src[:, n * b:n * b + n], wcol(s["w"]), start=True, stop=True)
                elif kind == "post":
                    pe.wait_ge(out_ready, CB * (s["phase"] - NCH + 1))
                    mm = pe.matmul(bank[:, :], wcol(s["w"]), oT[c][:, :], start=True, stop=True)
                elif kind == "up":
                    pe.wait_ge(xn_ready, s["norm"])
                    mm = pe.matmul(bank[:, :], wcol((s["layer"], f"up{s['j']}")), xn[:, :], start=True, stop=True)
                elif kind == "down":
                    for j in range(FF):
                        pe.wait_ge(hidden_ready, FF * s["mlp"] + j + 1)
                        mm = pe.matmul(bank[:, :], wcol((s["layer"], f"dn{j}")), hid[:, j, :], start=(j == 0), stop=(j == FF - 1))
                mm.then_inc(dense_full[use % 2], 1)

            def score(n):
                e, g, b = n // PHASE_QUADS, n % QUADS, n // QUADS % CB
                c, nk = e % NCH, nk_of(n)
                layer, own = ATTN[e // NCH]
                if g == 0:
                    pe.wait_ge(q_ready, n // QUADS + 1)
                    pe.wait_ge(k_ready, n // QUADS + 1)
                if n >= 3:
                    pe.wait_ge(exp_ready, n - 2)
                out = scores[n % 3][:, 0:4 * nk].rearrange("p (h k) -> p h k", h=4)
                masked = layer == 1
                mm = pe.matmul(out, qz[c][:, g, T * b:T * b + T], kbd[c][:, :, nk * b:nk * b + nk], start=True, stop=not masked)
                if masked and own:
                    mm = pe.matmul(out, identb[:, :], mb[:, None, :].to_broadcast([P, 4, T]), start=False, stop=True)
                elif masked:
                    bb = c * CB + b
                    mm = pe.matmul(out, identb[:, :], cb[:, bb:bb + 1, :].to_broadcast([P, 4, TC]), start=False, stop=True)
                mm.then_inc(scores_ready, 1)

            def turn(n):
                nk = nk_of(n)
                pe.wait_ge(exp_ready, n + 1)
                if n >= 2:
                    pe.wait_ge(probs_ready, n - 1)
                for i in range(4):
                    mm = pe.transpose(turned[n % 2][0:nk, 128 * i:128 * i + 128], weights_q[:, n % 3, nk * i:nk * i + nk], const("ident"))
                mm.then_inc(turned_ready, 1)

            def weigh(u):
                e, b = u // CB, u % CB
                c, nk = e % NCH, nk_of(u * QUADS)
                pe.wait_ge(probs_ready, QUADS * (u + 1))
                if b == 0:
                    pe.wait_ge(v_ready, e + 1)
                if u >= 1:
                    pe.wait_ge(out_ready, u)
                for i in range(4):
                    for g in range(QUADS):
                        pe.matmul(av[32 * g:32 * g + 32, 0:128], vpad[c][0:nk, b, g, i, :], probs[0:nk, u % 2, g, 128 * i:128 * i + 128],
                                  start=(i == 0), stop=(i == 3), skip_group_check=True)
                pe.wait_ge(inverse8_ready, u + 1)
                mm = pe.transpose(av[:, 128:256], inverse8[:, u % 2, :], const("ident"))
                mm.then_inc(av_ready, 1)

            first_steps = [s for slot in lists[0] for s in slot]
            rows_left = list(range(NR0, NR))
            for s in first_steps:
                step(s)
                if s["use"] == 0:
                    setup_layer0()
                here = MODS_AFTER.get(s["use"], 0)
                if here:
                    pe.wait_ge(mod0_ready, 1)
                    pe.wait_ge(wm_loaded[1], 16)
                    modulations(rows_left[:here])
                    rows_left = rows_left[here:]
            for n in range(3):
                score(n)
            if rows_left:
                modulations(rows_left)
            pe.wait_ge(consts_loaded[1], 16)
            for e in range(NE):
                for j in range(PHASE_QUADS):
                    n = e * PHASE_QUADS + j
                    turn(n)
                    if n + 3 < NQ:
                        score(n + 3)
                    for s in lists[e + 1][j]:
                        step(s)
                    if n % QUADS == 0 and n:
                        if n == QUADS:
                            pe.wait_ge(setup_done, 1)
                        weigh(n // QUADS - 1)
                    if n == 1:
                        setup_rest()

            def tail_post(h):
                pe.wait_ge(out_ready, NU - CB + 2 * (h + 1))
                pe.matmul(tail_bank(USE_POST + h), wcol((3, "xo")), half(oT[NCH - 1], h), start=True, stop=True).then_inc(tail_full, 1)

            tail_post(0)
            weigh(NU - 1)
            tail_post(1)
            for h in range(2):
                pe.wait_ge(tail_x, h + 1)
                pe.matmul(tail_bank(USE_CENTER + h), const("center"), tail_input(h), start=True, stop=True).then_inc(tail_full, 1)
            for b in range(2):
                pe.wait_ge(dense_empty[b], (dense_uses + 1 - b) // 2)
            for h in range(2):
                pe.wait_ge(tail_sq, h + 1)
                pe.matmul(tail_bank(USE_VAR + h), const("mean"), half(sq, h), start=True, stop=True).then_inc(tail_full, 1)
            for h in range(2):
                pe.wait_ge(tail_xn, h + 1)
                for j in range(FF):
                    k = USE_UP + h * FF + j
                    if k >= USE_UP + len(tail_banks):
                        pe.wait_ge(tail_hidden, k - len(tail_banks) - USE_UP + 1)
                    pe.matmul(tail_bank(k), wcol((3, f"up{j}")), half(xn, h), start=True, stop=True).then_inc(tail_full, 1)
            for h in range(2):
                pe.wait_ge(tail_hidden, USE_DOWN + h - len(tail_banks) - USE_UP + 1)
                for j in range(FF):
                    pe.wait_ge(tail_hidden, h * FF + j + 1)
                    mm = pe.matmul(tail_bank(USE_DOWN + h), wcol((3, f"dn{j}")), half(hid[:, j, :], h), start=(j == 0), stop=(j == FF - 1))
                mm.then_inc(tail_full, 1)

        @block.scalar
        def _(act):
            def step(s):
                kind, c = s["kind"], s["c"]
                if s.get("mode") in ("rope", "rope2", "any") or kind in ("post", "down"):
                    return
                use = s["use"]
                bank = dense[use % 2]
                if kind != "up" or s["j"] < FF - 1:
                    wait_dense_full(act, use)
                if kind == "center":
                    wd = width_of(s)
                    act.activation(sq[:, 0:wd], bank[:, 0:wd], ACT.Square).then_inc(sq_ready, 1)
                elif kind == "var":
                    wd = width_of(s)
                    eps = epst[:, 1:2] if s["eps"] == 1e-6 else epst[:, 0:1]
                    act.activation(lnv[:, 0:wd], bank[:, 0:wd], ACT.Ln, bias=eps).then_inc(dense_empty[use % 2], 1)
                    act.wait_ge(dense_empty[use % 2], use // 2 + 1)
                    if s["norm"]:
                        act.wait_ge(xhat_ready, s["norm"])
                    act.activation(rstd[:, 0:wd], lnv[:, 0:wd], ACT.Exp, scale=-0.5).then_inc(rstd_ready, 1)
                elif kind == "proj":
                    wd = s["width"]
                    bias = bc[:, BC[s["bias"]]:BC[s["bias"]] + 1]
                    dst = qraw if s["dst"] == "q" else kraw
                    if s["phase"]:
                        act.wait_ge(q_ready if s["dst"] == "q" else k_ready, CB * s["phase"])
                    act.activation(dst[:, 0:wd], bank[:, 0:wd], ACT.Identity, bias=bias).then_inc(dense_empty[use % 2], 1)
                    act.wait_ge(dense_empty[use % 2], use // 2 + 1)
                    act.sem_inc(qraw_ready if s["dst"] == "q" else kraw_ready, 1)
                elif kind == "v":
                    n = s["n"]
                    if s["phase"] < NCH:
                        act.wait_ge(vpad_zero, s["phase"] + 1)
                    else:
                        act.wait_ge(av_ready, CB * (s["phase"] - 1))
                    dst = diagonal(vpad[c][0:n, :, :, :, :].rearrange("p b g i r -> p (b g) (i r)"))
                    src = bank[0:n, :].rearrange("p (a i d) -> p a i d", i=4, d=HD)
                    act.activation(dst, src, ACT.Copy).then_inc(dense_empty[use % 2], 1)
                    act.wait_ge(dense_empty[use % 2], use // 2 + 1)
                    act.sem_inc(v_ready, 1)
                elif kind == "up":
                    layer, last = s["layer"], s["j"] == FF - 1
                    b1 = BC[f"L{layer}b1_{s['j']}"]
                    bias = bc[:, b1:b1 + 1]
                    if not last:
                        act.activation(hid[:, s["j"], :], bank[:, :], ACT.Identity, bias=bias).then_inc(dense_empty[use % 2], 1)
                        act.wait_ge(dense_empty[use % 2], use // 2 + 1)
                        act.sem_inc(hidden_raw, 1)
                        return
                    act.wait_ge(hidden_raw, (FF - 1) * (s["mlp"] + 1))
                    act.preload_act_table_set(GELU_SET if layer == 3 else GELU_TANH_SET)
                    gelu = ACT.Gelu if layer == 3 else ACT.Gelu_apprx_tanh
                    for j in range(FF - 1):
                        act.activation(hid[:, j, :], hid[:, j, :], gelu).then_inc(hidden_ready, 1)
                    wait_dense_full(act, use)
                    act.activation(hid[:, FF - 1, :], bank[:, :], gelu, bias=bias).then_inc(dense_empty[use % 2], 1)
                    act.preload_act_table_set(EXP_LN_SET)
                    act.wait_ge(dense_empty[use % 2], use // 2 + 1)
                    act.sem_inc(hidden_ready, 1)

            def diagonal(rows):
                return bass.AP(tensor=rows.tensor, offset=rows.offset, ap=[list(rows.ap[0]), list(rows.ap[1]), [32 + HD, 4], [1, HD]])

            def exps(n):
                nk, u = nk_of(n), n // QUADS
                act.wait_ge(max_ready, n + 1)
                if n >= 3:
                    act.wait_ge(turned_ready, n - 2)
                if n % QUADS == 0 and u >= 2:
                    act.wait_ge(inverse_ready, u - 1)
                for i in range(4):
                    h = 4 * (n % QUADS) + i
                    ins = act.activation(weights_q[:, n % 3, nk * i:nk * i + nk], scores[n % 3][:, nk * i:nk * i + nk], ACT.Exp,
                                         bias=rmax[:, n % 8, i:i + 1], accum_out=sums[:, u % 2, h:h + 1])
                ins.then_inc(exp_ready, 1)

            act.wait_ge(small_loaded, 16)
            act.activation(silu[:, :], cond, ACT.Silu).then_inc(silu_ready, 1)
            act.preload_act_table_set(EXP_LN_SET)
            act.wait_ge(eps_ready, 1)
            for slot in lists[0]:
                for s in slot:
                    step(s)
            exps(0)
            for e in range(NE):
                for j in range(PHASE_QUADS):
                    n = e * PHASE_QUADS + j
                    if n + 1 < NQ:
                        exps(n + 1)
                    for s in lists[e + 1][j]:
                        step(s)

            for h in range(2):
                act.wait_ge(tail_full, USE_CENTER + h + 1)
                act.activation(half(sq, h), tail_bank(USE_CENTER + h), ACT.Square).then_inc(tail_sq, 1)
            for h in range(2):
                act.wait_ge(tail_full, USE_VAR + h + 1)
                act.activation(half(lnv, h), tail_bank(USE_VAR + h), ACT.Ln, bias=epst[:, 0:1]).then_inc(tail_ln, 1)
                act.wait_ge(tail_ln, h + 1)
                act.activation(half(rstd, h), half(lnv, h), ACT.Exp, scale=-0.5).then_inc(tail_rstd, 1)
            act.preload_act_table_set(GELU_SET)
            for h in range(2):
                for j in range(FF):
                    b1 = BC[f"L3b1_{j}"]
                    act.wait_ge(tail_full, USE_UP + h * FF + j + 1)
                    act.activation(half(hid[:, j, :], h), tail_bank(USE_UP + h * FF + j), ACT.Gelu, bias=bc[:, b1:b1 + 1])\
                       .then_inc(tail_hidden, 1)

        @block.vector
        def _(dve):
            linked = [0]

            def link(ins):
                linked[0] += 1
                ins.then_inc(setup_chain, 1)
                dve.wait_ge(setup_chain, linked[0])

            def setup_layer0():
                dve.memset(epst[:, 0:1], 1e-5)
                link(dve.memset(epst[:, 1:2], 1e-6))
                dve.sem_inc(eps_ready, 1)
                dve.wait_ge(small_loaded, 16)
                dve.wait_ge(mod0_summed, 1)
                link(dve.tensor_tensor(mod[:, 0:NR0, :], av[:, 0:NR0 * B].rearrange("p (t b) -> p t b", b=B),
                                       bm[:, 0:NR0, None].to_broadcast([P, NR0, B]), ALU.add))
                link(dve.tensor_scalar(mod[:, 0:NM0, :], mod[:, 0:NM0, :], 1.0, None, ALU.add))
                dve.sem_inc(mod0_ready, 1)
                dve.wait_ge(consts_loaded[0], 16)

            def setup_masks():
                dve.wait_ge(masks_loaded, 4 * 16)
                dve.tensor_copy(mTf[:, :], mT8[:, :]).then_inc(masks_ready, 1)
                dve.tensor_copy(cmTf[:, :], cmT8[:, :]).then_inc(masks_ready, 1)
                dve.tensor_copy(mf[:, :], m8[:, :])
                link(dve.tensor_copy(cmf[:, :, :], cm8[:, :].rearrange("p (b k) -> p b k", b=B)))
                dve.wait_ge(consts_loaded[1], 16)
                link(dve.tensor_copy(identb[:, :], const("ident")))
                link(dve.tensor_reduce(anyr[:, :], mf[:, :], AX_X, ALU.max))
                link(dve.tensor_scalar(noany[:, :], anyr[:, :], -1.0, 1.0, ALU.mult, ALU.add))
                link(dve.tensor_scalar(mf[:, :], mf[:, :], noany[:, 0:1], -1.0, ALU.max, ALU.add))
                link(dve.tensor_scalar(mb[:, :], mf[:, :], BIG, None, ALU.mult))

            def setup_rest():
                dve.wait_ge(tables_summed, 1)
                link(dve.tensor_scalar(anyq[:, :], av[:, 256:256 + T], 1.0, None, ALU.min))
                link(dve.tensor_scalar(anyc[:, :], av[:, 256 + T:256 + T + B], 1.0, None, ALU.min))
                dve.tensor_tensor(cosq[:, :], const("cos2"), anyq[:, :], ALU.mult)
                link(dve.tensor_tensor(sinq[:, :], const("sin2"), anyq[:, :], ALU.mult))
                link(dve.tensor_scalar(noanyc[:, :], anyc[:, :], -1.0, 1.0, ALU.mult, ALU.add))
                link(dve.tensor_tensor(cmf[:, :, :], cmf[:, :, :], noanyc[:, :, None].to_broadcast([P, B, TC]), ALU.max))
                link(dve.tensor_scalar(cb[:, :, :], cmf[:, :, :], -1.0, BIG, ALU.add, ALU.mult))
                link(dve.tensor_tensor(mod[:, NR0:NR, :], av[:, NR0 * B:NR * B].rearrange("p (t b) -> p t b", b=B),
                                       bm[:, NR0:NR, None].to_broadcast([P, NR - NR0, B]), ALU.add))
                scales = mod[:, NR0:NR0 + NM - NM0, :]
                link(dve.scalar_tensor_tensor(out=scales, in0=scales, scalar=1.0,
                                              in1=nwt[:, :, None].to_broadcast([P, NM - NM0, B]), op0=ALU.add, op1=ALU.mult))
                for t, bias in enumerate(["L0bp", "L2bproj", "L2bcp"]):
                    link(dve.tensor_tensor(pcol[:, t:t + 1], av[:, NR * B + t:NR * B + t + 1], bc[:, BC[bias]:BC[bias] + 1], ALU.add))
                dve.sem_inc(setup_done, 1)

            def spread(dst, raw, mask, nt, ready):
                for b in range(CB):
                    dve.tensor_tensor(dst[:, :, nt * b:nt * b + nt], raw[:, None, nt * b:nt * b + nt].to_broadcast([P, 4, nt]),
                                      mask[:, :, None].to_broadcast([P, 4, nt]), ALU.mult).then_inc(ready, 1)

            def step(s):
                kind, c, mode = s["kind"], s["c"], s.get("mode")
                if kind == "var":
                    wd = width_of(s)
                    per = wd // CB
                    use = s["use"] - 1
                    dve.wait_ge(rstd_ready, s["norm"] + 1)
                    if s["xn_reader"] >= 0:
                        wait_dense_full(dve, s["xn_reader"])
                    plain = s["mod"] is None
                    dst = xn if plain else xhat
                    dve.tensor_tensor(dst[:, 0:wd], dense[use % 2][:, 0:wd], rstd[:, 0:wd], ALU.mult).then_inc(dense_empty[use % 2], 1)
                    dve.wait_ge(dense_empty[use % 2], use // 2 + 1)
                    dve.sem_inc(xhat_ready, 1)
                    if plain:
                        dve.sem_inc(xn_ready, 1)
                        return
                    scale, shift = ROW[("scale", s["mod"])], ROW[("shift", s["mod"])]
                    for b in range(CB):
                        bb = c * CB + b
                        ins = dve.tensor_scalar(xn[:, per * b:per * b + per], xhat[:, per * b:per * b + per],
                                                mod[:, scale, bb:bb + 1], mod[:, shift, bb:bb + 1], ALU.mult, ALU.add)
                    ins.then_inc(xn_ready, 1)
                    return
                if kind in ("post", "down"):
                    use = s["use"]
                    bank, xs = dense[use % 2], chunk("x", c)
                    wait_dense_full(dve, use)
                    if s["gate"] is None:
                        dve.scalar_tensor_tensor(out=xs, in0=bank[:, :], scalar=post_bias(s), in1=xs, op0=ALU.add, op1=ALU.add)\
                           .then_inc(dense_empty[use % 2], 1)
                        dve.wait_ge(dense_empty[use % 2], use // 2 + 1)
                        dve.sem_inc(x_ready, 1)
                        return
                    gates = mod[:, ROW[("gate", s["gate"])], c * CB:(c + 1) * CB, None].to_broadcast([P, CB, T])
                    dve.scalar_tensor_tensor(out=delta[:, :].rearrange("p (b t) -> p b t", b=CB), in0=bank[:, :].rearrange("p (b t) -> p b t", b=CB),
                                             scalar=post_bias(s), in1=gates, op0=ALU.add, op1=ALU.mult).then_inc(dense_empty[use % 2], 1)
                    dve.wait_ge(dense_empty[use % 2], use // 2 + 1)
                    dve.tensor_tensor(xs, xs, delta[:, :], ALU.add).then_inc(x_ready, 1)
                    return
                if kind != "proj":
                    return
                if s["dst"] == "k" and mode == "bias":
                    dve.wait_ge(kraw_ready, s["raw"] + 1)
                    spread(kbd[c], kraw, const("headmask"), s["width"] // CB, k_ready)
                if mode == "bias":
                    return
                use = s["use"]
                bank = dense[use % 2]
                wait_dense_full(dve, use)
                if mode == "any":
                    dve.wait_ge(q_ready, CB * s["phase"])
                    dve.tensor_tensor(qraw[:, :].rearrange("p (b t) -> p b t", b=CB), bank[:, :].rearrange("p (b t) -> p b t", b=CB),
                                      anyc[:, c * CB:(c + 1) * CB, None].to_broadcast([P, CB, T]), ALU.mult).then_inc(dense_empty[use % 2], 1)
                    dve.wait_ge(dense_empty[use % 2], use // 2 + 1)
                    dve.sem_inc(qraw_ready, 1)
                    return
                wd, period = s["width"], s["period"]
                if mode == "rope" and s["rope"]:
                    dve.wait_ge(rope_summed, s["rope"])
                dst = ropea if mode == "rope" else ropeb
                t = tab(s["tabs"][mode == "rope2"])[:, 0:period]
                dve.tensor_tensor(dst[:, 0:wd].rearrange("p (b t) -> p b t", t=period), bank[:, 0:wd].rearrange("p (b t) -> p b t", t=period),
                                  t[:, None, :].to_broadcast([P, CB, period]), ALU.mult).then_inc(dense_empty[use % 2], 1)
                dve.wait_ge(dense_empty[use % 2], use // 2 + 1)
                dve.sem_inc(rope_halves, 1)
                if mode == "rope2" and s["dst"] == "k":
                    if s["phase"]:
                        dve.wait_ge(k_ready, CB * s["phase"])
                    dve.tensor_tensor(kraw[:, 0:wd], ropea[:, 0:wd], ropeb[:, 0:wd], ALU.add).then_inc(rope_summed, 1)
                    dve.wait_ge(rope_summed, s["rope"] + 1)
                    spread(kbd[c], kraw, const("headmask"), period, k_ready)

            def row_max(n):
                nk = nk_of(n)
                dve.wait_ge(scores_ready, n + 1)
                dve.tensor_reduce(rmax[:, n % 8, :], scores[n % 3][:, 0:4 * nk].rearrange("p (h k) -> p h k", h=4),
                                  AX_X, ALU.max, negate=True).then_inc(max_ready, 1)

            def fetch(n):
                nk, u = nk_of(n), n // QUADS
                dve.wait_ge(turned_ready, n + 1)
                if n % QUADS == 0 and u >= 2:
                    dve.wait_ge(av_ready, u - 1)
                dve.tensor_copy(probs[0:nk, u % 2, n % QUADS, :], turned[n % 2][0:nk, :]).then_inc(probs_ready, 1)

            def invert(u):
                dve.wait_ge(exp_ready, QUADS * (u + 1))
                if u >= 2:
                    dve.wait_ge(av_ready, u - 1)
                if u >= 1:
                    dve.wait_ge(inverse8_ready, u)
                dve.reciprocal(inverse[:, :], sums[:, u % 2, :]).then_inc(inverse_ready, 1)
                dve.wait_ge(inverse_ready, u + 1)
                dve.tensor_copy(inverse8[:, u % 2, :].rearrange("p (h d) -> p h d", d=HD), inverse[:, :, None].to_broadcast([P, H, HD]))\
                   .then_inc(inverse8_ready, 1)

            def divide(u):
                e, b = u // CB, u % CB
                dve.wait_ge(av_ready, u + 1)
                if u >= 1:
                    dve.wait_ge(out_ready, u)
                dve.tensor_copy(inverseT[:, :], av[:, 128:256]).then_inc(inverseT_ready, 1)
                dve.wait_ge(inverseT_ready, u + 1)
                dve.tensor_tensor(oT[e % NCH][:, T * b:T * b + T], av[:, 0:128], inverseT[:, :], ALU.mult).then_inc(out_ready, 1)

            setup_layer0()
            for slot in lists[0]:
                for s in slot:
                    step(s)
            row_max(0)
            row_max(1)
            for e in range(NE):
                for j in range(PHASE_QUADS):
                    n = e * PHASE_QUADS + j
                    if n:
                        fetch(n - 1)
                    if n + 2 < NQ:
                        row_max(n + 2)
                    if n % QUADS == 0 and n:
                        invert(n // QUADS - 1)
                    if n:
                        for s in lists[(n - 1) // PHASE_QUADS + 1][(n - 1) % PHASE_QUADS]:
                            step(s)
                    if n == 1:
                        setup_masks()
                    if n == 3:
                        setup_rest()
                    if n % QUADS == DIVIDE_SLOT and n > QUADS:
                        divide(n // QUADS - 1)
            for s in lists[NE][PHASE_QUADS - 1]:
                step(s)
            fetch(NQ - 1)
            invert(NU - 1)

            def tail_post(h):
                dve.wait_ge(tail_full, USE_POST + h + 1)
                dve.tensor_tensor(tail_input(h), tail_bank(USE_POST + h), tail_input(h), ALU.add).then_inc(tail_x, 1)

            tail_post(0)
            divide(NU - 1)
            tail_post(1)
            scale, shift = ROW[("scale", "L3n3")], ROW[("shift", "L3n3")]
            for h in range(2):
                dve.wait_ge(tail_rstd, h + 1)
                dve.tensor_tensor(half(xhat, h), tail_bank(USE_CENTER + h), half(rstd, h), ALU.mult).then_inc(tail_xhat, 1)
                dve.wait_ge(tail_xhat, h + 1)
                for b in (2 * h, 2 * h + 1):
                    bb = (NCH - 1) * CB + b
                    ins = dve.tensor_scalar(xn[:, T * b:T * b + T], xhat[:, T * b:T * b + T], mod[:, scale, bb:bb + 1], mod[:, shift, bb:bb + 1],
                                            ALU.mult, ALU.add)
                ins.then_inc(tail_xn, 1)
            for h in range(2):
                dve.wait_ge(tail_full, USE_DOWN + h + 1)
                dve.scalar_tensor_tensor(out=tail_input(h), in0=tail_bank(USE_DOWN + h), scalar=bc[:, BC["L3b2"]:BC["L3b2"] + 1], in1=tail_input(h),
                                         op0=ALU.add, op1=ALU.add).then_inc(tail_x, 1)

        @block.gpsimd
        def _(pool):
            def step(s):
                if s["kind"] != "proj" or s["dst"] != "q" or s["mode"] == "rope":
                    return
                c = s["c"]
                if s["mode"] == "rope2":
                    pool.wait_ge(rope_halves, 2 * (s["rope"] + 1))
                    if s["phase"]:
                        pool.wait_ge(q_ready, CB * s["phase"])
                    pool.tensor_tensor(qraw[:, :], ropea[:, :], ropeb[:, :], ALU.add).then_inc(rope_summed, 1)
                    pool.wait_ge(rope_summed, s["rope"] + 1)
                else:
                    pool.wait_ge(qraw_ready, s["raw"] + 1)
                for b in range(CB):
                    pool.tensor_tensor(qz[c][:, :, T * b:T * b + T], qraw[:, None, T * b:T * b + T].to_broadcast([P, QUADS, T]),
                                       const("groupscale")[:, :, None].to_broadcast([P, QUADS, T]), ALU.mult).then_inc(q_ready, 1)

            for c in range(NCH):
                pool.memset(vpad[c][:, :, :, :, :], 0.0).then_inc(vpad_zero, 1)
            pool.wait_ge(consts_loaded[0], 16)
            for slots in lists:
                for slot in slots:
                    for s in slot:
                        step(s)


def host_consts():
    p = np.arange(P)
    h, d = p // HD, p % HD
    inv = (1.0 / 10000.0 ** (np.arange(0, HD, 2, dtype=np.float32) / HD)).astype(np.float32)
    ang = (np.arange(T, dtype=np.float32)[None, :] * inv[d % 4][:, None]).astype(np.float32)
    cos, sin = np.cos(ang).astype(np.float32), np.sin(ang).astype(np.float32)
    sin = np.where((d < 4)[:, None], -sin, sin).astype(np.float32)
    half = T // 2
    parts = {
        "center": np.eye(P, dtype=np.float32) - np.float32(1.0 / D),
        "mean": np.full((P, P), 1.0 / D, np.float32),
        "ident": np.eye(P, dtype=np.float32),
        "ones": np.ones((P, P), np.float32),
        "headmask": (h[:, None] % 4 == np.arange(4)[None, :]).astype(np.float32),
        "groupscale": (h[:, None] // 4 == np.arange(4)[None, :]).astype(np.float32) * np.float32(SCALE),
        "cos": cos, "sin": sin,
        "cos2": np.concatenate([cos[:, :half]] * 2, 1), "sin2": np.concatenate([sin[:, :half]] * 2, 1),
    }
    return np.concatenate([parts[n] for n in CONSTS], 1)


def kernel(**inputs):
    import concourse.bacc as bacc
    from concourse.bass_utils import run_bass_kernel_spmd

    g = {n: np.asarray(v) for n, v in inputs.items()}
    L0, L1, L2, L3 = ({n[9:]: v for n, v in g.items() if n.startswith(f"L{l}_xcond_")} for l in range(4))

    def cols(wt, i, size=128):
        return wt[:, size * i:size * i + size]

    def swapped(wt):
        return wt.reshape(wt.shape[0], H, 2, HD // 2)[:, :, ::-1, :].reshape(wt.shape[0], H * HD)

    aw, mw = L1["adaLN_W"], L2["W_mod"]
    ab, mb_ = L1["adaLN_b"].reshape(9, 128).T, L2["b_mod"].reshape(6, 128).T
    lw = {n: L3[f"ln{n}_w"].T for n in (1, 2, 3)}
    lb = {n: L3[f"ln{n}_b"].reshape(2, 128).T for n in (1, 2, 3)}

    def both(half):
        one, six = (1, 0)[half], (1, 0)[half]
        ws = [cols(L0["Wss_q"], half), cols(L0["Wss_kv"], half), cols(aw, one), cols(aw, 3 + one), cols(aw, 6 + one),
              cols(mw, six), cols(mw, 3 + six)] + [cols(lw[n], half) for n in (1, 2, 3)]
        bs = [L0["bss_q"].reshape(2, 128).T[:, half], L0["bss_kv"].reshape(2, 128).T[:, half], ab[:, one], ab[:, 3 + one], ab[:, 6 + one],
              mb_[:, six], mb_[:, 3 + six]] + [lb[n][:, half] for n in (1, 2, 3)]
        return ws, bs

    sw, sbias = both(0)
    hw, hbias = both(1)
    gw = [cols(aw, 2), cols(aw, 5), cols(aw, 8), cols(mw, 2), cols(mw, 5)]
    gbias = [ab[:, 2], ab[:, 5], ab[:, 8], mb_[:, 2], mb_[:, 5]]
    one = np.ones(128, np.float32)

    def rope_qkv(wt, names):
        return {names[0]: cols(wt, 0), names[0] + "r": swapped(cols(wt, 0)), names[1]: cols(wt, 1), names[1] + "r": swapped(cols(wt, 1)), names[2]: cols(wt, 2)}

    def mlp(up, down):
        return {**{f"up{j}": cols(up, j) for j in range(FF)}, **{f"dn{j}": down[128 * j:128 * j + 128] for j in range(FF)}}

    wl = {
        0: dict(q=L0["Wq"], k=cols(L0["Wkv"], 0), v=cols(L0["Wkv"], 1), o=L0["Wp"]),
        1: dict(**rope_qkv(L1["qkv_W"], ("sq", "sk", "sv")), so=L1["attn_out_W"], xq=L1["cq_W"], xk=L1["ck_W"], xv=L1["cv_W"],
                xo=L1["co_W"], **mlp(L1["mlp_W1"], L1["mlp_W2"])),
        2: dict(sq=cols(L2["W_qkv"], 0), sk=cols(L2["W_qkv"], 1), sv=cols(L2["W_qkv"], 2), so=L2["W_proj"], xq=L2["W_qc"],
                xk=cols(L2["W_kvc"], 0), xv=cols(L2["W_kvc"], 1), xo=L2["W_cproj"], **mlp(L2["W_mlp1"], L2["W_mlp2"])),
        3: dict(**rope_qkv(L3["qkv_w"].T, ("sq", "sk", "sv")), so=L3["sa_out_w"].T, xq=L3["q_w"].T, xqr=swapped(L3["q_w"].T),
                xk=L3["k_w"].T, xkr=swapped(L3["k_w"].T), xv=L3["v_w"].T, xo=L3["ca_out_w"].T, **mlp(L3["ffn_w1"].T, L3["ffn_w2"].T)),
    }
    b_of = {"zero": np.zeros(128, np.float32), "L0bq": L0["bq"], "L0bk": L0["bkv"][:128], "L0bv": L0["bkv"][128:], "L0bp": L0["bp"],
            "L2bq": L2["b_qkv"][:128], "L2bk": L2["b_qkv"][128:256], "L2bv": L2["b_qkv"][256:], "L2bproj": L2["b_proj"],
            "L2bqc": L2["b_qc"], "L2bkc": L2["b_kvc"][:128], "L2bvc": L2["b_kvc"][128:], "L2bcp": L2["b_cproj"],
            "L1b2": L1["mlp_b2"], "L2b2": L2["b_mlp2"], "L3b2": L3["ffn_b2"]}
    for l, v in ((1, L1["mlp_b1"]), (2, L2["b_mlp1"]), (3, L3["ffn_b1"])):
        for j in range(FF):
            b_of[f"L{l}b1_{j}"] = v[128 * j:128 * j + 128]

    def rows(of_scale, of_shift, of_gate):
        return of_scale[:NM0] + of_shift[:NM0] + of_scale[NM0:] + of_shift[NM0:] + of_gate

    small = [g["cond_1024"].T, np.stack(rows(sbias, hbias, gbias), 1), np.stack([L1["norm1_w"], L1["normc_w"], L1["norm2_w"]] + [one] * 5, 1),
             np.stack([b_of[n] for n in BCOLS], 1)]
    arrays = {
        "xT": g["x"].reshape(B * T, D).T,
        "ctxT": g["ctx_1024"].reshape(B * TC, D).T,
        "small": np.concatenate(small, 1),
        "wmod": np.concatenate(rows(sw, hw, gw), 1),
        "weights": np.concatenate([wl[l][n] for l in WBLOCKS for n in WBLOCKS[l]], 1),
        "consts": host_consts(),
        "mask": g["mask_SxS_bk0"],
        "maskT": g["mask_SxS_bk0"].T,
        "cmaskT": g["mask_BxS2_bf1"].T,
        "cmask": g["mask_BxS2_bf1"].reshape(1, B * TC),
    }
    arrays = {n: np.ascontiguousarray(v) for n, v in arrays.items()}
    nc = bacc.Bacc("TRN2", target_bir_lowering=False, num_devices=1)
    args = [nc.dram_tensor(f"{n}_dram", v.shape, mybir.dt.from_np(v.dtype), kind="ExternalInput").ap() for n, v in arrays.items()]
    out = nc.dram_tensor("outT_dram", [D, B * T], F32, kind="ExternalOutput").ap()
    blocks_kernel(nc, *args, out)
    r = run_bass_kernel_spmd(nc, [{f"{n}_dram": v for n, v in arrays.items()}], core_ids=[0])
    return np.ascontiguousarray(r.results[0]["outT_dram"].T).reshape(B, T, D)
```
